# Optimizing a Trainium2 kernel written in Bass

```python
import numpy as np
import jax
import jax.numpy as jnp

def _softmax(x, axis=-1):
    return jax.nn.softmax(x, axis=axis)

def _gelu(x):
    return jax.nn.gelu(x, approximate=True)

def _silu(x):
    return jax.nn.silu(x)

def _sigmoid(x):
    return jax.nn.sigmoid(x)

def _layernorm(x, axis=-1, eps=1e-05):
    m = jnp.mean(x, axis=axis, keepdims=True)
    v = jnp.var(x, axis=axis, keepdims=True)
    return (x - m) / jnp.sqrt(v + eps)

def _scatter_add(tgt, idx, src, axis=0):
    return tgt.at[idx].add(src)

def _segment_sum(src, seg, n):
    return jax.ops.segment_sum(src, seg, n)
kernel_name = 'mk_seq_postln_d1_jaxref_r8_1f3d50'

def setup_inputs(seed: int=0):
    np.random.seed(seed)
    _w = jnp.asarray

    def _L0_attn_setup():
        import jax, jax.numpy as jnp
        import numpy as np
        B, T, D = (2, 256, 128)
        H = 8
        KD = 128
        VD = 32
        KEY_DIM = H * KD
        VAL_DIM = H * VD
        KS = 4
        EPS_NORM = 1e-06
        EPS_RMS = 1e-05

        def _xavier(key, shape):
            fan_in, fan_out = (shape[0], shape[1])
            lim = np.sqrt(6.0 / (fan_in + fan_out))
            return jax.random.uniform(key, shape, jnp.float32, -lim, lim)

        def _causal_dw_conv_silu(x, w):
            C = x.shape[-1]
            y = jax.lax.conv_general_dilated(jnp.swapaxes(x, 1, 2), w[:, None, :], window_strides=(1,), padding=[(KS - 1, 0)], feature_group_count=C)
            return jax.nn.silu(jnp.swapaxes(y, 1, 2))

        def _l2norm(x):
            n = jnp.sqrt(jnp.sum(x * x, axis=-1, keepdims=True))
            return x / jnp.maximum(n, EPS_NORM)

        def _gdn_forward(x, Wq, Wk, Wv, Wa, Wb, Wg, Wo, A_log, dt_bias, conv_q, conv_k, conv_v, o_norm_w):
            bsz, seq_len, _ = x.shape
            beta = jax.nn.sigmoid(x @ Wb) * 2.0
            g = -jnp.exp(A_log)[None, None, :] * jax.nn.softplus(x @ Wa + dt_bias[None, None, :])
            alpha = jnp.exp(g)
            q = _causal_dw_conv_silu(x @ Wq, conv_q).reshape(bsz, seq_len, H, KD)
            k = _causal_dw_conv_silu(x @ Wk, conv_k).reshape(bsz, seq_len, H, KD)
            v = _causal_dw_conv_silu(x @ Wv, conv_v).reshape(bsz, seq_len, H, VD)
            q = _l2norm(q)
            k = _l2norm(k)
            qT = jnp.swapaxes(q, 0, 1)
            kT = jnp.swapaxes(k, 0, 1)
            vT = jnp.swapaxes(v, 0, 1)
            aT = jnp.swapaxes(alpha, 0, 1)
            bT = jnp.swapaxes(beta, 0, 1)

            def step(state, inp):
                q_t, k_t, v_t, a_t, b_t = inp
                retained = jnp.einsum('bhvk,bhk->bhv', state, k_t)
                a4 = a_t[..., None, None]
                b4 = b_t[..., None, None]
                rk = retained[..., None] * k_t[:, :, None, :]
                vk = v_t[..., None] * k_t[:, :, None, :]
                state = a4 * (state - b4 * rk) + b4 * vk
                o_t = jnp.einsum('bhvk,bhk->bhv', state, q_t)
                return (state, o_t)
            state0 = jnp.zeros((bsz, H, VD, KD), jnp.float32)
            _, outT = jax.lax.scan(step, state0, (qT, kT, vT, aT, bT))
            out = jnp.swapaxes(outT, 0, 1)
            gate = (x @ Wg).reshape(bsz, seq_len, H, VD)
            rms = jax.lax.rsqrt(jnp.mean(out * out, axis=-1, keepdims=True) + EPS_RMS)
            out = out * rms * o_norm_w * jax.nn.silu(gate)
            out = out.reshape(bsz, seq_len, VAL_DIM)
            return out @ Wo
        key = jax.random.key(seed)
        ks = jax.random.split(key, 16)
        x = jax.random.normal(ks[0], (B, T, D), jnp.float32)
        Wq = _xavier(ks[1], (D, KEY_DIM))
        Wk = _xavier(ks[2], (D, KEY_DIM))
        Wv = _xavier(ks[3], (D, VAL_DIM))
        Wa = _xavier(ks[4], (D, H))
        Wb = _xavier(ks[5], (D, H))
        Wg = _xavier(ks[6], (D, VAL_DIM))
        Wo = _xavier(ks[7], (VAL_DIM, D))
        A_log = jnp.log(jax.random.uniform(ks[8], (H,), jnp.float32, 0.5, 16.0))
        dt = jnp.exp(jax.random.uniform(ks[9], (H,), jnp.float32, np.log(0.001), np.log(0.1)))
        dt = jnp.clip(dt, 0.0001, None)
        dt_bias = dt + jnp.log(-jnp.expm1(-dt))

        def conv_w(k, c):
            lim = np.sqrt(6.0 / (1 + KS))
            return jax.random.uniform(k, (c, KS), jnp.float32, -lim, lim)
        conv_q = conv_w(ks[10], KEY_DIM)
        conv_k = conv_w(ks[11], KEY_DIM)
        conv_v = conv_w(ks[12], VAL_DIM)
        o_norm_w = jnp.ones((VD,), jnp.float32)
        return dict(x=x, Wq=Wq, Wk=Wk, Wv=Wv, Wa=Wa, Wb=Wb, Wg=Wg, Wo=Wo, A_log=A_log, dt_bias=dt_bias, conv_q=conv_q, conv_k=conv_k, conv_v=conv_v, o_norm_w=o_norm_w)
    _L0_attn_in = _L0_attn_setup()

    def _L0_ffn_setup():
        import jax, jax.numpy as jnp
        import numpy as np
        import math
        D_IN = 128
        FEATURES = (512, 512, 128)
        BATCH, SEQ = (8, 256)

        def _conn_dense(kernel_bool, x):
            w = jnp.where(kernel_bool, jnp.float32(1.0), jnp.float32(-1.0))
            return x @ w
        key = jax.random.key(seed)
        kx, kk0, kk1, kk2 = jax.random.split(key, 4)
        x = jax.random.normal(kx, (BATCH, SEQ, D_IN), dtype=jnp.float32)
        k0 = jax.random.randint(kk0, (2 * D_IN, FEATURES[0]), 0, 2).astype(jnp.bool_)
        k1 = jax.random.randint(kk1, (FEATURES[0], FEATURES[1]), 0, 2).astype(jnp.bool_)
        k2 = jax.random.randint(kk2, (FEATURES[1], FEATURES[2]), 0, 2).astype(jnp.bool_)
        s0 = jnp.asarray(1.0 / math.sqrt(2 * D_IN), dtype=jnp.float32)
        s1 = jnp.asarray(1.0 / math.sqrt(FEATURES[0]), dtype=jnp.float32)
        s2 = jnp.asarray(1.0 / math.sqrt(FEATURES[1]), dtype=jnp.float32)
        return {'x': x, 'k0': k0, 'k1': k1, 'k2': k2, 's0': s0, 's1': s1, 's2': s2}
    _L0_ffn_in = _L0_ffn_setup()
    _d = {'L0_attn_x': _L0_attn_in['x'], 'L0_attn_Wq': _L0_attn_in['Wq'], 'L0_attn_Wk': _L0_attn_in['Wk'], 'L0_attn_Wv': _L0_attn_in['Wv'], 'L0_attn_Wa': _L0_attn_in['Wa'], 'L0_attn_Wb': _L0_attn_in['Wb'], 'L0_attn_Wg': _L0_attn_in['Wg'], 'L0_attn_Wo': _L0_attn_in['Wo'], 'L0_attn_A_log': _L0_attn_in['A_log'], 'L0_attn_dt_bias': _L0_attn_in['dt_bias'], 'L0_attn_conv_q': _L0_attn_in['conv_q'], 'L0_attn_conv_k': _L0_attn_in['conv_k'], 'L0_attn_conv_v': _L0_attn_in['conv_v'], 'L0_attn_o_norm_w': _L0_attn_in['o_norm_w'], 'L0_ffn_k0': _L0_ffn_in['k0'], 'L0_ffn_k1': _L0_ffn_in['k1'], 'L0_ffn_k2': _L0_ffn_in['k2'], 'L0_ffn_s0': _L0_ffn_in['s0'], 'L0_ffn_s1': _L0_ffn_in['s1'], 'L0_ffn_s2': _L0_ffn_in['s2']}
    _x0 = _d['L0_attn_x']
    _d['L0_attn_x'] = jax.random.normal(jax.random.fold_in(jax.random.key(seed), 1), (1, 2048, 128), dtype=_x0.dtype)
    del _x0
    return _d

def reference(L0_attn_x, L0_attn_Wq, L0_attn_Wk, L0_attn_Wv, L0_attn_Wa, L0_attn_Wb, L0_attn_Wg, L0_attn_Wo, L0_attn_A_log, L0_attn_dt_bias, L0_attn_conv_q, L0_attn_conv_k, L0_attn_conv_v, L0_attn_o_norm_w, L0_ffn_k0, L0_ffn_k1, L0_ffn_k2, L0_ffn_s0, L0_ffn_s1, L0_ffn_s2):

    def _L0_attn_ref(x, Wq, Wk, Wv, Wa, Wb, Wg, Wo, A_log, dt_bias, conv_q, conv_k, conv_v, o_norm_w):
        import jax, jax.numpy as jnp
        import numpy as np
        B, T, D = (2, 256, 128)
        H = 8
        KD = 128
        VD = 32
        KEY_DIM = H * KD
        VAL_DIM = H * VD
        KS = 4
        EPS_NORM = 1e-06
        EPS_RMS = 1e-05

        def _xavier(key, shape):
            fan_in, fan_out = (shape[0], shape[1])
            lim = np.sqrt(6.0 / (fan_in + fan_out))
            return jax.random.uniform(key, shape, jnp.float32, -lim, lim)

        def _causal_dw_conv_silu(x, w):
            C = x.shape[-1]
            y = jax.lax.conv_general_dilated(jnp.swapaxes(x, 1, 2), w[:, None, :], window_strides=(1,), padding=[(KS - 1, 0)], feature_group_count=C)
            return jax.nn.silu(jnp.swapaxes(y, 1, 2))

        def _l2norm(x):
            n = jnp.sqrt(jnp.sum(x * x, axis=-1, keepdims=True))
            return x / jnp.maximum(n, EPS_NORM)

        def _gdn_forward(x, Wq, Wk, Wv, Wa, Wb, Wg, Wo, A_log, dt_bias, conv_q, conv_k, conv_v, o_norm_w):
            bsz, seq_len, _ = x.shape
            beta = jax.nn.sigmoid(x @ Wb) * 2.0
            g = -jnp.exp(A_log)[None, None, :] * jax.nn.softplus(x @ Wa + dt_bias[None, None, :])
            alpha = jnp.exp(g)
            q = _causal_dw_conv_silu(x @ Wq, conv_q).reshape(bsz, seq_len, H, KD)
            k = _causal_dw_conv_silu(x @ Wk, conv_k).reshape(bsz, seq_len, H, KD)
            v = _causal_dw_conv_silu(x @ Wv, conv_v).reshape(bsz, seq_len, H, VD)
            q = _l2norm(q)
            k = _l2norm(k)
            qT = jnp.swapaxes(q, 0, 1)
            kT = jnp.swapaxes(k, 0, 1)
            vT = jnp.swapaxes(v, 0, 1)
            aT = jnp.swapaxes(alpha, 0, 1)
            bT = jnp.swapaxes(beta, 0, 1)

            def step(state, inp):
                q_t, k_t, v_t, a_t, b_t = inp
                retained = jnp.einsum('bhvk,bhk->bhv', state, k_t)
                a4 = a_t[..., None, None]
                b4 = b_t[..., None, None]
                rk = retained[..., None] * k_t[:, :, None, :]
                vk = v_t[..., None] * k_t[:, :, None, :]
                state = a4 * (state - b4 * rk) + b4 * vk
                o_t = jnp.einsum('bhvk,bhk->bhv', state, q_t)
                return (state, o_t)
            state0 = jnp.zeros((bsz, H, VD, KD), jnp.float32)
            _, outT = jax.lax.scan(step, state0, (qT, kT, vT, aT, bT))
            out = jnp.swapaxes(outT, 0, 1)
            gate = (x @ Wg).reshape(bsz, seq_len, H, VD)
            rms = jax.lax.rsqrt(jnp.mean(out * out, axis=-1, keepdims=True) + EPS_RMS)
            out = out * rms * o_norm_w * jax.nn.silu(gate)
            out = out.reshape(bsz, seq_len, VAL_DIM)
            return out @ Wo
        return _gdn_forward(x, Wq, Wk, Wv, Wa, Wb, Wg, Wo, A_log, dt_bias, conv_q, conv_k, conv_v, o_norm_w)

    def _L0_ffn_ref(x, k0, k1, k2, s0, s1, s2):
        import jax, jax.numpy as jnp
        import numpy as np
        import math
        D_IN = 128
        FEATURES = (512, 512, 128)
        BATCH, SEQ = (8, 256)

        def _conn_dense(kernel_bool, x):
            w = jnp.where(kernel_bool, jnp.float32(1.0), jnp.float32(-1.0))
            return x @ w
        h = jnp.concatenate([x, -x], axis=-1)
        h = s0 * _conn_dense(k0, h)
        h = jax.nn.relu(h) * 2
        h = s1 * _conn_dense(k1, h)
        h = jax.nn.relu(h) * 2
        h = s2 * _conn_dense(k2, h)
        return h
    x = L0_attn_x
    x = _layernorm(x + _L0_attn_ref(x, L0_attn_Wq, L0_attn_Wk, L0_attn_Wv, L0_attn_Wa, L0_attn_Wb, L0_attn_Wg, L0_attn_Wo, L0_attn_A_log, L0_attn_dt_bias, L0_attn_conv_q, L0_attn_conv_k, L0_attn_conv_v, L0_attn_o_norm_w), axis=-1)
    x = _layernorm(x + _L0_ffn_ref(x, L0_ffn_k0, L0_ffn_k1, L0_ffn_k2, L0_ffn_s0, L0_ffn_s1, L0_ffn_s2), axis=-1)
    return x

_drawn_inputs = setup_inputs


def setup_inputs(seed=0):
    import zlib

    import numpy as np

    out = dict(_drawn_inputs(seed))
    spreads = {'L0_attn_o_norm_w': (1.0, 0.2)}
    factors = {}
    for name, (base, spread) in spreads.items():
        noise = np.random.default_rng([zlib.crc32(name.encode()), seed]).standard_normal(out[name].shape)
        drawn = base * np.exp(spread * noise) if base else spread * noise
        out[name] = jnp.asarray(drawn.astype(out[name].dtype))
    for name, factor in factors.items():
        out[name] = (out[name] * factor).astype(out[name].dtype)
    return out
```

```python
from contextlib import ExitStack

import concourse.bass as bass
from concourse import mybir

F32 = mybir.dt.float32
F16 = mybir.dt.float16
U8 = mybir.dt.uint8
ALU = mybir.AluOpType
ACT = mybir.ActivationFunctionType
AX = mybir.AxisListType

P = 128
C = 64
B = 32
GT = 512
TPG = GT // P
CPG = GT // C
TAPS = 4
EPS = 1e-5
NEG = -1e30
EARLY = 16
LN_EXP = "natural_log_exp_and_others"
LN2 = 0.6931471805599453


def weave(a, b):
    at = sorted([((k + 0.5) / len(a), 0, k) for k in range(len(a))] + [((k + 0.5) / len(b), 1, k) for k in range(len(b))])
    return [(a, b)[which][k] for _, which, k in at]


def order(groups, heads):
    def project(s):
        if s >= groups:
            return []
        out = []
        for i in range(2 * heads):
            out.append(("proj", s, i))
            if i >= 2:
                out.append(("norm2", s, i - 2))
        out += [("norm2", s, i) for i in (2 * heads - 2, 2 * heads - 1)]
        return out + [("proj", s, i) for i in (2 * heads, 2 * heads + 1)] + [("gate", s, jj) for jj in range(TPG // 2)]

    def solve_for(s):
        first = [("logs", s, 0)] + [("vals", s, jj) for jj in range(TPG // 2)]
        for j in range(TPG):
            first.append(("decay", s, j))
            for hh in range(2):
                first.append(("scores", s, 2 * j + hh))
        first.append(("units", s, 0))
        second = [("invert", s, t) for t in range(1, B)] + [("blocks", s, 0)]
        third = []
        for j in range(TPG):
            third += [("turn", s, j), ("cross1", s, j), ("cross2", s, j)]
        return first, second, third

    def recur(s, cs):
        out = []
        for c in cs:
            if c % 2 == 0:
                out += [("keys", s, c), ("keys", s, c + 1)]
            out += [("read", s, c), ("solve", s, c), ("state", s, c), ("outs", s, c)]
        return out

    def finish(s, j):
        return [(name, s, j) for name in ("rms", "mix", "ln1", "up", "mid", "down")]

    def prepare(s):
        if s >= groups:
            return []
        first, second, third = solve_for(s)
        ahead = project(s + 1)[:EARLY]
        if s > 0:
            first = first[:3] + weave(first[3:], finish(s - 1, TPG - 1))
        return first + (weave(second, ahead) if ahead else second) + third

    steps = project(0) + [("cum", 0, 0)] + prepare(0)
    for s in range(groups):
        ahead = project(s + 1)[EARLY:]
        n = -(-len(ahead) // TPG)
        for j in range(TPG):
            part = ahead[j * n:(j + 1) * n] + (finish(s, j - 1) if j else [])
            if j and len(ahead):
                part = weave(ahead[j * n:(j + 1) * n], finish(s, j - 1))
            steps += weave(recur(s, (2 * j, 2 * j + 1)), part) if part else recur(s, (2 * j, 2 * j + 1))
        steps += prepare(s + 1)
    return steps + finish(groups - 1, TPG - 1)


def post_ln_block(nc, x, Wq, Wk, Wv, Wa, Wb, Wg, Wo, A_log, dt_bias, conv_q, conv_k, conv_v, o_norm_w,
                  k0, k1, k2, s0, s1, s2, out):
    T, D = x.shape
    H = A_log.shape[0]
    VD = Wv.shape[1] // H
    HV = H * VD
    F = k1.shape[0]
    assert D == P and Wq.shape[1] == H * P and HV == 2 * P and F == 4 * P and T % GT == 0
    NT = T // P
    NG = T // GT
    NP = 2 * H + 2
    HH = H // 2

    steps = order(NG, H)
    ring_use = {}
    for st in steps:
        name, s, i = st
        if name in ("gate", "vals", "decay", "scores", "cross1", "cross2", "keys", "mix", "ln1", "up", "mid", "down"):
            ring_use[st] = len(ring_use)
            if name == "mix":
                ring_use[("mix2", s, i)] = len(ring_use)
    ring_steps = list(ring_use)

    with ExitStack() as ctx:
        def sb(name, shape, dt=F32):
            return ctx.enter_context(nc.sbuf_tensor(name, shape, dt))

        def sem(name):
            return ctx.enter_context(nc.semaphore(name))

        bank = [ctx.enter_context(nc.psum_tensor(f"bank{i}", [P, 512], F32)) for i in range(8)]
        proj_bank, ring_bank, norm_bank = bank[0:2], (bank[2], bank[3], bank[6]), bank[7]
        taps_bank = (bank[7], bank[5])
        read_ps = bank[4][:, 0:HV]
        state_ps = bank[4][:, HV:2 * HV]
        solve_ps = bank[5][:, 0:HV]
        outs_ps = bank[5][:, HV:2 * HV]

        ident = sb("ident", [P, P])
        ones = sb("ones", [P, 1])
        eps = sb("eps", [P, 1])
        same_chunk = sb("same_chunk", [P, P])
        tri = sb("tri", [P, C])
        later = sb("later", [P, C])
        w_taps = sb("w_taps", [P, NP, TAPS, P])
        wg = sb("wg", [P, HV])
        wab = sb("wab", [P, 2 * H])
        wo = sb("wo", [P, 2, P])
        bias_ab = sb("bias_ab", [P, 2 * H])
        neg_a = sb("neg_a", [P, H])
        onw = sb("onw", [P, VD])
        s_in = sb("s_in", [P, 3])
        s_work = sb("s_work", [P, 6])
        w0 = sb("w0", [P, F], F16)
        w1 = sb("w1", [P, 4, F], F16)
        w2 = sb("w2", [P, 4, P], F16)

        xT = sb("xT", [P, TAPS - 1 + T])
        g = sb("g", [P, NT * H])
        lnb = sb("lnb", [P, NT * H])
        decay_kq = sb("decay_kq", [P, 2, NT * H])
        decay_end = sb("decay_end", [P, 2, NT * H])

        kq = [sb(f"kq{i}", [P, H, TPG, 4 * C]) for i in range(2)]
        sq = sb("sq", [P, 2, GT])
        vT = sq
        lnn = sb("lnn", [P, 2, TPG * H])
        norm_k = sb("norm_k", [P, TPG * H])
        inv_q = [sb(f"inv_q{i}", [P, TPG * H]) for i in range(2)]
        cneg = sb("cneg", [P, TPG * H])
        g_tri = sb("g_tri", [P, H, C])
        dec = sb("dec", [P, 2, H, C])
        dend = sb("dend", [P, TPG, H])
        nmat = sb("nmat", [P, TPG, H, C])
        amat = sb("amat", [P, TPG, H, C])
        unit = sb("unit", [P, B, B])
        prod = sb("prod", [P, B * B])
        umat = sb("umat", [P, TPG, H, C])
        t11 = sb("t11", [P, H, B])
        z21 = sb("z21", [P, H, B])
        nv = sb("nv", [P, TPG, HV])
        gate = [sb(f"gate{i}", [P, TPG, HV]) for i in range(2)]
        keyd = sb("keyd", [P, 2, H, P])
        state = sb("state", [P, 2, HV])
        state_g = sb("state_g", [P, HV])
        gpk = sb("gpk", [P, HV])
        gpq = sb("gpq", [P, HV])
        rhs = sb("rhs", [P, HV])
        sol = sb("sol", [P, HV])
        o_t = sb("o_t", [P, TPG, HV])
        osq = gpk
        oss = sb("oss", [P, H])
        orms = sb("orms", [P, H])
        oT = sb("oT", [P, 2, P])
        xres = sb("xres", [P, 2, P])
        x1 = sb("x1", [P, P])
        stats = sb("stats", [P, 6])
        mv = sb("mv", [P, 2])
        rstd = sb("rstd", [P, 1])
        xn = sb("xn", [P, 2, P])
        xh = sb("xh", [P, 2, P], F16)
        h1 = sb("h1", [P, 2, F], F16)
        h2 = sb("h2", [P, 2, F], F16)
        x3 = x1
        fin = sb("fin", [P, 2, P])

        x_in = nmat[:, :, :, :].rearrange("p a h t -> p (a h t)").rearrange("p (n d) -> p n d", d=P)
        upto = keyd[:, 0, 0, :]
        in_chunk = keyd[:, 0, 1:3, :]
        tri_kq = keyd[:, 0, 3:5, :].rearrange("p a (w t) -> p a w t", w=2)
        wqk_raw = umat[:, :, :, :].rearrange("p n h t -> p (n h t)").rearrange("p (w d) -> p w d", w=2)
        wv_raw = t11[:, :, :].rearrange("p h t -> p (h t)")
        tap_rows = kq[1][0:1].rearrange("p h n t -> p (h n t)").rearrange("p (w d) -> p w d", w=2)
        tap_row_v = prod[0:1, :]
        ones_row = in_chunk[0:1, 0, :]
        k_raw = unit[:, :, :].rearrange("p i t -> p (i t)").bitcast(U8)
        k0_raw = k_raw[:, 0:2 * F].rearrange("p (a f) -> p a f", a=2)
        k1_raw = k_raw[:, 2 * F:6 * F].rearrange("p (a f) -> p a f", a=4)
        k2_raw = k_raw[:, 6 * F:6 * F + 4 * P].rearrange("p (a f) -> p a f", a=4)
        pre = amat[:, 0, :, :].rearrange("p h t -> p (h t)")[:, 0:2 * NT * H]
        mag = amat[:, 1, :, :].rearrange("p h t -> p (h t)")[:, 0:2 * NT * H]
        lnp = amat[:, 2, :, :].rearrange("p h t -> p (h t)")[:, 0:2 * NT * H]
        w0_raw = amat[:, 3, :, :].rearrange("p h t -> p (h t)").bitcast(F16).rearrange("p (a f) -> p a f", a=2)

        scratch = nc.dram_tensor("scratch", (2, 2, P, B * B), F32, kind="Internal").ap()

        ld_x = [sem(f"ld_x{q}") for q in range(4)]
        ld_w, ld_small, ld_mlp = sem("ld_w"), sem("ld_small"), sem("ld_mlp")
        consts = sem("consts")
        pool_done = sem("pool_done")
        dve_done = sem("dve_done")
        act_done = sem("act_done")
        xt_ps, xt_done = sem("xt_ps"), sem("xt_done")
        z_ps, cum_ps = sem("z_ps"), sem("cum_ps")
        mag_done, lnp_done, g_done, lnb_done, dg_done = (sem("mag_done"), sem("lnp_done"), sem("g_done"),
                                                         sem("lnb_done"), sem("dg_done"))
        ea_done, mlpw_done, sgn_done = sem("ea_done"), sem("mlpw_done"), sem("sgn_done")
        proj_done, taps_ps, wtap_done = sem("proj_done"), sem("taps_ps"), sem("wtap_done")
        silu_done, sq_done, n2_done = sem("silu_done"), sem("sq_done"), sem("n2_done")
        ring_done = sem("ring_done")
        n2_max, log_done, norms_done, cneg_done = sem("n2_max"), sem("log_done"), sem("norms_done"), sem("cneg_done")
        gate_act, gate_done = sem("gate_act"), sem("gate_done")
        gtri_done, dmask_done, darg_done, dec_done, dend_done = (sem("gtri_done"), sem("dmask_done"),
                                                                 sem("darg_done"), sem("dec_done"), sem("dend_done"))
        scores_done = sem("scores_done")
        unit_out, unit_in, block_out, block_in = sem("unit_out"), sem("unit_in"), sem("block_out"), sem("block_in")
        inv_step = sem("inv_step")
        t11_done, z21_done, u12_done, nv_done = sem("t11_done"), sem("z21_done"), sem("u12_done"), sem("nv_done")
        zero_done = sem("zero_done")
        keyd_done = sem("keyd_done")
        read_done, gp_step, rhs_done = sem("read_done"), sem("gp_step"), sem("rhs_done")
        solve_done, sol_done, state_mm, state_done, stateg_done = (sem("solve_done"), sem("sol_done"),
                                                                   sem("state_mm"), sem("state_done"),
                                                                   sem("stateg_done"))
        outs_done, o_done = sem("outs_done"), sem("o_done")
        rms_step, rms_ln, rms_done, o_ready = sem("rms_step"), sem("rms_ln"), sem("rms_done"), sem("o_ready")
        ot_done, ln_step, ln_ln, rstd_done, xn_done = (sem("ot_done"), sem("ln_step"),
                                                                sem("ln_ln"), sem("rstd_done"), sem("xn_done"))
        xh_done, xlo_done, h_hi, h_lo = sem("xh_done"), sem("xlo_done"), sem("h_hi"), sem("h_lo")
        y_step, y_ln, y_rstd, fin_done = sem("y_step"), sem("y_ln"), sem("y_rstd"), sem("fin_done")
        xres_in = [sem(f"xres_in{i}") for i in range(2)]
        stored = [sem(f"stored{i}") for i in range(2)]

        NCONST = 12
        N_SMALL, N_W, N_MLP = 9, 6, 3

        def tile_heads(ap, tile):
            return ap[:, tile * H:(tile + 1) * H]

        def keys_of(buf, h):
            return buf[:, h, :, C:3 * C]

        def queries_of(buf, h):
            return buf[:, h, :, :].rearrange("p n (a t) -> p n a t", a=4)[:, :, 0:4:3, :]

        def over(ap, n):
            return ap.unsqueeze(len(ap.shape)).to_broadcast(list(ap.shape) + [n])

        def heads(ap):
            return ap.rearrange("p (h v) -> p h v", v=VD)

        def wait_ring(eng, step):
            eng.wait_ge(ring_done, ring_use[step] + 1)
            return ring_bank[ring_use[step] % 3]

        def bank_read(step):
            name, s, i = step
            tile = TPG * s + i
            return {"gate": (gate_act, TPG // 2 * s + i + 1),
                    "vals": (nv_done, TPG // 2 * s + i + 1), "decay": (darg_done, tile + 1),
                    "scores": (scores_done, 2 * TPG * s + i + 1), "keys": (keyd_done, 2 * TPG * s + i + 1),
                    "cross1": (z21_done, tile + 1), "cross2": (u12_done, tile + 1),
                    "mix": (ot_done, tile + 1), "mix2": (ln_step, 3 * tile + 1), "ln1": (xlo_done, tile + 1),
                    "up": (h_lo, 2 * tile + 1), "mid": (h_lo, 2 * tile + 2), "down": (y_step, 3 * tile + 1)}[name]

        block = ctx.enter_context(nc.Block())

        @block.sync
        def _(sp):
            for q in range(4):
                sp.dma_start(x_in[:, 4 * q:4 * q + 4, :],
                             x[4 * q * P:(4 * q + 4) * P, :].rearrange("(n p) d -> p n d", p=P)).then_inc(ld_x[q], 16)
            sp.dma_start(wab[:, 0:H], Wa).then_inc(ld_small, 16)
            sp.dma_start(wab[:, H:2 * H], Wb).then_inc(ld_small, 16)
            sp.dma_start(bias_ab[:, 0:H], dt_bias.partition_broadcast(P)).then_inc(ld_small, 16)
            sp.dma_start(neg_a[:, :], A_log.partition_broadcast(P)).then_inc(ld_small, 16)
            sp.dma_start(onw[:, :], o_norm_w.partition_broadcast(P)).then_inc(ld_small, 16)
            for w, (weight, conv) in enumerate(((Wk, conv_k), (Wq, conv_q))):
                sp.dma_start(tap_rows[:, w, :], conv.rearrange("(o c) j -> o (c j)", o=1)).then_inc(ld_w, 16)
                sp.dma_start(wqk_raw[:, w, :], weight).then_inc(ld_w, 16)
            sp.dma_start(tap_row_v, conv_v.rearrange("(o c) j -> o (c j)", o=1)).then_inc(ld_w, 16)
            sp.dma_start(wv_raw, Wv).then_inc(ld_w, 16)
            sp.dma_start(wg[:, :], Wg).then_inc(ld_small, 16)
            for n, s_n in enumerate((s0, s1, s2)):
                sp.dma_start(s_in[:, n:n + 1], s_n.partition_broadcast(P)).then_inc(ld_small, 16)
            sp.dma_start(k0_raw, k0.rearrange("(a p) f -> p a f", p=P)).then_inc(ld_mlp, 16)
            sp.dma_start(k1_raw, k1.rearrange("(a p) f -> p a f", p=P)).then_inc(ld_mlp, 16)
            sp.dma_start(k2_raw, k2.rearrange("(a p) f -> p a f", p=P)).then_inc(ld_mlp, 16)
            sp.dma_start(wo[:, :, :], Wo.rearrange("(a p) n -> p a n", p=P)).then_inc(ld_small, 16)

            def to_units(s, j):
                sp.wait_ge(scores_done, 2 * (TPG * s + j) + 2)
                for b in range(4):
                    u = (4 * j + b) * H
                    sp.dma_start(scratch[0, s % 2, u:u + H, :].rearrange("h (i t) -> i h t", t=B),
                                 nmat[b * B:(b + 1) * B, j, :, b % 2 * B:(b % 2 + 1) * B]).then_inc(unit_out, 16)

            for name, s, i in steps:
                if name == "scores" and i % 2:
                    to_units(s, i // 2)
                elif name == "units":
                    sp.wait_ge(unit_out, 16 * 4 * TPG * (s + 1))
                    if s == 0:
                        sp.wait_ge(mlpw_done, 1)
                    else:
                        sp.wait_ge(block_out, 16 * s)
                    sp.dma_start(unit[:, :, :].rearrange("p i t -> p (i t)"), scratch[0, s % 2]).then_inc(unit_in, 16)
                elif name == "blocks":
                    sp.wait_ge(inv_step, 63 * (s + 1))
                    sp.dma_start(scratch[1, s % 2], unit[:, :, :].rearrange("p i t -> p (i t)")).then_inc(block_out, 16)
                    sp.wait_ge(block_out, 16 * (s + 1))
                    if s >= 1:
                        sp.wait_ge(solve_done, CPG * s)
                    sp.wait_ge(zero_done, 1)
                    for j in range(TPG):
                        for b in range(4):
                            u = (4 * j + b) * H
                            sp.dma_start(umat[b * B:(b + 1) * B, j, :, b % 2 * B:(b % 2 + 1) * B],
                                         scratch[1, s % 2, u:u + H, :].rearrange("h (i t) -> i h t", t=B)
                                         ).then_inc(block_in, 16)
                elif name == "rms":
                    tile = TPG * s + i
                    if tile >= 2:
                        sp.wait_ge(ln_step, 3 * (tile - 2) + 1)
                    sp.dma_start(xres[:, tile % 2, :], x[tile * P:(tile + 1) * P, :]).then_inc(xres_in[tile % 2], 16)
                elif name == "down":
                    tile = TPG * s + i
                    sp.wait_ge(fin_done, tile + 1)
                    sp.dma_start(out[tile * P:(tile + 1) * P, :], fin[:, tile % 2, :]).then_inc(stored[tile % 2], 16)
            for i in range(2):
                sp.wait_ge(stored[i], 16 * NT // 2)
            sp.wait_ge(unit_out, 16 * 4 * TPG * NG)
            sp.wait_ge(block_out, 16 * NG)

        @block.gpsimd
        def _(pool):
            n_done = [0]

            def then_next(ins):
                n_done[0] += 1
                ins.then_inc(pool_done, 1)
                pool.wait_ge(pool_done, n_done[0])

            nc.gpsimd.memset(ones[:, :], 1.0)
            nc.gpsimd.memset(eps[:, :], EPS)
            nc.gpsimd.memset(xT[:, 0:TAPS - 1], 0.0)
            nc.gpsimd.memset(bias_ab[:, H:2 * H], 0.0)
            nc.gpsimd.memset(state[:, 0, :], 0.0)
            nc.gpsimd.memset(later[:, :], 0.0)
            nc.gpsimd.memset(tri[:, :], 1.0)
            nc.gpsimd.memset(same_chunk[:, :], 0.0)
            nc.gpsimd.memset(tri_kq, 0.0)
            nc.gpsimd.memset(in_chunk, 0.0)
            then_next(nc.gpsimd.memset(ident[:, :], 0.0))
            nc.gpsimd.affine_select(out=ident[:, :], in_=ident[:, :], compare_op=ALU.not_equal, fill=1.0, base=0,
                                    pattern=[[-1, P]], channel_multiplier=1).then_inc(consts, 1)
            for a in range(2):
                half = slice(C * a, C * a + C)
                nc.gpsimd.memset(same_chunk[half, half], 1.0)
                nc.gpsimd.memset(in_chunk[half, a, :], 1.0)
                nc.gpsimd.affine_select(out=tri[half, :], in_=tri[half, :], compare_op=ALU.is_ge, fill=0.0, base=0,
                                        pattern=[[1, C]], channel_multiplier=-1)
                then_next(nc.gpsimd.affine_select(out=later[half, :], in_=later[half, :], compare_op=ALU.is_ge,
                                                  fill=NEG, base=0, pattern=[[1, C]], channel_multiplier=-1))
            then_next(nc.gpsimd.affine_select(out=upto, in_=same_chunk[:, :], compare_op=ALU.is_ge, fill=0.0, base=0,
                                              pattern=[[1, P]], channel_multiplier=-1))
            for a in range(2):
                half = slice(C * a, C * a + C)
                for w in range(2):
                    last = nc.gpsimd.tensor_copy(tri_kq[half, a, w, :], tri[half, :])
                if a == 0:
                    then_next(last)
            last.then_inc(consts, 1)
            pool.wait_ge(consts, 2)
            pool.wait_ge(wtap_done, NP)
            nc.gpsimd.memset(umat[:, :, :, :], 0.0).then_inc(zero_done, 1)

            def mlp_weights():
                pool.wait_ge(ld_mlp, 16 * N_MLP)
                pool.wait_ge(sgn_done, 1)
                pool.wait_ge(dg_done, 1)
                then_next(nc.gpsimd.tensor_scalar(w0_raw, k0_raw, 2.0, None, ALU.mult))
                then_next(nc.gpsimd.tensor_tensor(w0[:, :], w0_raw[:, 0, :], w0_raw[:, 1, :], ALU.subtract))
                nc.gpsimd.tensor_scalar(w2[:, :, :], k2_raw, 2.0, -1.0, ALU.mult, ALU.add)
                then_next(nc.gpsimd.tensor_scalar(w1[:, :, :], k1_raw, 2.0, -1.0, ALU.mult, ALU.add))
                nc.gpsimd.tensor_scalar(w0[:, :], w0[:, :], s_work[:, 1:2], None, ALU.mult)
                nc.gpsimd.tensor_scalar(w1[:, :, :], w1[:, :, :], s_work[:, 3:4], None, ALU.mult
                                        ).then_inc(mlpw_done, 1)

            def squares(s, i):
                if i >= 2 * H:
                    return
                m, w = i // 2, i % 2
                pool.wait_ge(silu_done, NP * s + i + 1)
                if i >= 2:
                    pool.wait_ge(n2_done, 2 * H * s + i - 1)
                elif s > 0:
                    pool.wait_ge(ring_done, ring_use[("vals", s - 1, 1)] + 1)
                if w == 0:
                    src, dst = keys_of(kq[s % 2], m), sq[:, w, :].rearrange("p (n t) -> p n t", t=P)
                else:
                    src, dst = queries_of(kq[s % 2], m), sq[:, w, :].rearrange("p (n a t) -> p n a t", a=2, t=C)
                nc.gpsimd.tensor_tensor(dst, src, src, ALU.mult).then_inc(sq_done, 1)

            def gates(s, jj):
                pool.wait_ge(gate_act, TPG // 2 * s + jj + 1)
                both = gate[s % 2][:, 2 * jj:2 * jj + 2, :].rearrange("p a (h v) -> p (a h) v", v=VD)
                nc.gpsimd.tensor_tensor(both, both, onw[:, :].unsqueeze(1).to_broadcast([P, 2 * H, VD]), ALU.mult
                                        ).then_inc(gate_done, 1)

            def decay(s, j):
                tile = TPG * s + j
                if tile >= 1:
                    pool.wait_ge(darg_done, tile)
                nc.gpsimd.tensor_tensor(g_tri[:, :, :], over(tile_heads(g, tile), C),
                                        tri[:, :].unsqueeze(1).to_broadcast([P, H, C]), ALU.mult
                                        ).then_inc(gtri_done, 1)
                pool.wait_ge(cneg_done, s + 1)
                if tile >= 2:
                    pool.wait_ge(scores_done, 2 * (tile - 1))
                    pool.wait_ge(dend_done, tile - 1)
                nc.gpsimd.tensor_tensor(dec[:, tile % 2], over(tile_heads(cneg, j), C),
                                        later[:, :].unsqueeze(1).to_broadcast([P, H, C]), ALU.add
                                        ).then_inc(dmask_done, 1)

            def stateg(c):
                if c > 0:
                    pool.wait_ge(state_done, c)
                nc.gpsimd.tensor_tensor(heads(state_g[:, :]), heads(state[:, c % 2, :]),
                                        over(tile_heads(decay_end[:, c % 2], c // 2), VD), ALU.mult
                                        ).then_inc(stateg_done, 1)

            for name, s, i in steps:
                if name == "proj":
                    squares(s, i)
                elif name == "gate":
                    gates(s, i)
                elif name == "decay":
                    decay(s, i)
                elif name == "logs" and s == 0:
                    mlp_weights()
                elif name == "read":
                    stateg(CPG * s + i)

        @block.scalar
        def _(act):
            nc.scalar.preload_act_table_set(LN_EXP)
            for q in range(4):
                act.wait_ge(xt_ps, q + 1)
                nc.scalar.activation(xT[:, TAPS - 1 + 512 * q:TAPS - 1 + 512 * q + 512], bank[q][:, :], ACT.Copy).then_inc(xt_done, 1)
            act.wait_ge(ld_small, 16 * N_SMALL + 16)
            nc.scalar.activation(neg_a[:, :], neg_a[:, :], ACT.Exp).then_inc(ea_done, 1)
            act.wait_ge(mag_done, 1)
            nc.scalar.activation(mag, mag, ACT.Exp).then_inc(mag_done, 1)
            act.wait_ge(mag_done, 2)
            nc.scalar.activation(lnp, mag, ACT.Ln, bias=1.0).then_inc(lnp_done, 1)
            def cum():
                act.wait_ge(cum_ps, 1)
                nc.scalar.preload_act_table_set(LN_EXP)
                nc.scalar.activation(decay_kq[:, :, :], bank[5][:, P:3 * P].rearrange("p (a n) -> p a n", a=2), ACT.Exp)
                nc.scalar.activation(decay_end[:, :, :], bank[6][:, 0:2 * P].rearrange("p (a n) -> p a n", a=2),
                                     ACT.Exp).then_inc(dg_done, 1)

            def proj(s, i):
                n = NP * s + i
                m, w = i // 2, i % 2
                act.wait_ge(proj_done, n + 1)
                ps = proj_bank[w][:, :]
                if m == H:
                    act.wait_ge(n2_done, 2 * H * s + 2 * H - 1 + w)
                    nc.scalar.activation(vT[:, w, :], ps, ACT.Silu).then_inc(silu_done, 1)
                    return
                if s >= 2:
                    act.wait_ge(read_done, CPG * (s - 1))
                elif s == 1:
                    act.wait_ge(taps_ps, NP)
                if w == 0:
                    nc.scalar.activation(keys_of(kq[s % 2], m), ps.rearrange("p (n t) -> p n t", t=P), ACT.Silu
                                         ).then_inc(silu_done, 1)
                else:
                    nc.scalar.activation(queries_of(kq[s % 2], m), ps.rearrange("p (n a t) -> p n a t", a=2, t=C),
                                         ACT.Silu).then_inc(silu_done, 1)

            def gates(s, jj):
                ps = wait_ring(act, ("gate", s, jj))
                if s >= 2:
                    act.wait_ge(o_ready, TPG * (s - 1))
                nc.scalar.activation(gate[s % 2][:, 2 * jj:2 * jj + 2, :],
                                                ps[:, :].rearrange("p (a n) -> p a n", a=2), ACT.Silu
                                                ).then_inc(gate_act, 1)

            def logs(s):
                nc.scalar.preload_act_table_set(LN_EXP)
                act.wait_ge(n2_max, s + 1)
                if s >= 1:
                    act.wait_ge(cneg_done, s)
                nc.scalar.activation(lnn[:, :, :], lnn[:, :, :], ACT.Ln).then_inc(log_done, 1)
                act.wait_ge(log_done, s + 1)
                if s >= 1:
                    act.wait_ge(nv_done, TPG // 2 * s)
                if s >= 2:
                    act.wait_ge(rms_step, 3 * TPG * (s - 1))
                nc.scalar.activation(norm_k[:, :], lnn[:, 0, :], ACT.Exp, scale=0.5)
                nc.scalar.activation(inv_q[s % 2][:, :], lnn[:, 1, :], ACT.Exp, scale=-0.5).then_inc(norms_done, 1)

            def decay(s, j):
                tile = TPG * s + j
                act.wait_ge(darg_done, tile + 1)
                nc.scalar.activation(dec[:, tile % 2], dec[:, tile % 2], ACT.Exp).then_inc(dec_done, 1)
                act.wait_ge(dec_done, tile + 1)
                if s >= 1:
                    act.wait_ge(keyd_done, 2 * TPG * s)
                nc.scalar.activation(dend[:, j, :], dec[:, tile % 2, :, C - 1], ACT.Copy).then_inc(dend_done, 1)

            def cross1(s, j):
                tile = TPG * s + j
                ps = wait_ring(act, ("cross1", s, j))
                if tile >= 1:
                    act.wait_ge(ring_done, ring_use[("cross2", (tile - 1) // TPG, (tile - 1) % TPG)] + 1)
                for a in range(2):
                    rows = slice(C * a + B, C * a + C)
                    last = nc.scalar.activation(z21[rows], ps[rows, 0:HV].rearrange("p (h t) -> p h t", t=B), ACT.Copy)
                last.then_inc(z21_done, 1)

            def cross2(s, j):
                ps = wait_ring(act, ("cross2", s, j))
                for a in range(2):
                    rows = slice(C * a, C * a + B)
                    last = nc.scalar.activation(umat[rows, j, :, B:C],
                                                ps[rows, 0:HV].rearrange("p (h t) -> p h t", t=B), ACT.Copy,
                                                scale=-1.0)
                last.then_inc(u12_done, 1)

            def solve(s, i):
                c = CPG * s + i
                rows = slice(C * (c % 2), C * (c % 2) + C)
                act.wait_ge(solve_done, c + 1)
                if c >= 2:
                    act.wait_ge(outs_done, c - 1)
                nc.scalar.activation(sol[rows, :], solve_ps[rows, :], ACT.Copy).then_inc(sol_done, 1)

            def rms(s, j):
                tile = TPG * s + j
                nc.scalar.preload_act_table_set(LN_EXP)
                act.wait_ge(rms_step, 3 * tile + 3)
                nc.scalar.activation(orms[:, :], oss[:, :], ACT.Ln, scale=1.0 / VD, bias=eps[:, 0:1]
                                     ).then_inc(rms_ln, 1)
                act.wait_ge(rms_ln, tile + 1)
                nc.scalar.activation(orms[:, :], orms[:, :], ACT.Exp, scale=-0.5).then_inc(rms_done, 1)

            def mix(s, j):
                tile = TPG * s + j
                ps = wait_ring(act, ("mix", s, j))
                if tile >= 1:
                    act.wait_ge(ring_done, ring_use[("mix2", (tile - 1) // TPG, (tile - 1) % TPG)] + 1)
                nc.scalar.activation(oT[:, :, :], ps[:, 0:HV].rearrange("p (a t) -> p a t", a=2), ACT.Copy
                                                ).then_inc(ot_done, 1)
                nc.scalar.preload_act_table_set(LN_EXP)
                act.wait_ge(ln_step, 3 * tile + 3)
                nc.scalar.activation(rstd[:, :], mv[:, 1:2], ACT.Ln, bias=eps[:, 0:1]).then_inc(ln_ln, 1)
                act.wait_ge(ln_ln, tile + 1)
                nc.scalar.activation(rstd[:, :], rstd[:, :], ACT.Exp, scale=-0.5).then_inc(rstd_done, 1)

            def ln1(s, j):
                tile = TPG * s + j
                ps = wait_ring(act, ("ln1", s, j))
                if tile >= 1:
                    act.wait_ge(ring_done, ring_use[("up", (tile - 1) // TPG, (tile - 1) % TPG)] + 1)
                nc.scalar.activation(xh[:, 0, :], ps[:, 0:P], ACT.Copy).then_inc(xh_done, 1)

            def up(s, j):
                tile = TPG * s + j
                ps = wait_ring(act, ("up", s, j))
                if tile >= 1:
                    act.wait_ge(ring_done, ring_use[("mid", (tile - 1) // TPG, (tile - 1) % TPG)] + 1)
                nc.scalar.activation(h1[:, 0, :], ps[:, :], ACT.Relu).then_inc(h_hi, 1)

            def mid(s, j):
                tile = TPG * s + j
                ps = wait_ring(act, ("mid", s, j))
                if tile >= 1:
                    act.wait_ge(ring_done, ring_use[("down", (tile - 1) // TPG, (tile - 1) % TPG)] + 1)
                nc.scalar.activation(h2[:, 0, :], ps[:, :], ACT.Relu).then_inc(h_hi, 1)

            def down(s, j):
                tile = TPG * s + j
                nc.scalar.preload_act_table_set(LN_EXP)
                act.wait_ge(y_step, 3 * tile + 3)
                nc.scalar.activation(rstd[:, :], mv[:, 1:2], ACT.Ln, bias=eps[:, 0:1]).then_inc(y_ln, 1)
                act.wait_ge(y_ln, tile + 1)
                nc.scalar.activation(rstd[:, :], rstd[:, :], ACT.Exp, scale=-0.5).then_inc(y_rstd, 1)

            do = {"proj": proj, "gate": gates, "decay": decay, "cross1": cross1, "cross2": cross2,
                  "solve": solve, "rms": rms, "mix": mix, "ln1": ln1, "up": up, "mid": mid, "down": down}
            for name, s, i in steps:
                if name == "logs":
                    logs(s)
                elif name == "cum":
                    cum()
                elif name in do:
                    do[name](s, i)

        @block.vector
        def _(dve):
            n_done = [0]

            def then_next(ins):
                n_done[0] += 1
                ins.then_inc(dve_done, 1)
                dve.wait_ge(dve_done, n_done[0])

            vec = nc.vector
            dve.wait_ge(ld_small, 16 * N_SMALL + 16)
            for n in range(2):
                vec.scalar_tensor_tensor(out=s_work[:, 2 * n:2 * n + 1], in0=s_in[:, n:n + 1], scalar=-1.0,
                                         in1=s_in[:, n:n + 1], op0=ALU.mult, op1=ALU.max)
                then_next(vec.tensor_scalar(s_work[:, 2 * n + 1:2 * n + 2], s_in[:, n:n + 1], 0.0, 2.0, ALU.is_ge,
                                            ALU.mult))
            vec.tensor_scalar(s_work[:, 1:2], s_work[:, 1:2], -1.0, None, ALU.add)
            then_next(vec.tensor_scalar(s_work[:, 3:4], s_work[:, 3:4], -1.0, 1.0 / 16, ALU.add, ALU.mult))
            then_next(vec.tensor_scalar(s_work[:, 4:5], s_work[:, 0:1], s_work[:, 2:3], 64.0, ALU.mult, ALU.mult))
            vec.tensor_scalar(s_work[:, 5:6], s_work[:, 4:5], s_in[:, 2:3], None, ALU.mult).then_inc(sgn_done, 1)

            dve.wait_ge(consts, 2)
            dve.wait_ge(z_ps, 1)
            then_next(vec.tensor_tensor(pre.rearrange("p (n k) -> p n k", k=2 * H),
                                        bank[4][:, 0:2 * NT * H].rearrange("p (n k) -> p n k", k=2 * H),
                                        bias_ab[:, :].unsqueeze(1).to_broadcast([P, NT, 2 * H]), ALU.add))
            vec.scalar_tensor_tensor(out=mag, in0=pre, scalar=-1.0, in1=pre, op0=ALU.mult, op1=ALU.min
                                     ).then_inc(mag_done, 1)
            dve.wait_ge(ld_w, 16 * N_W)
            for i in range(NP):
                m, w = i // 2, i % 2
                src = wqk_raw[:, w, m * P:(m + 1) * P] if m < H else wv_raw[:, w * P:(w + 1) * P]
                dve.wait_ge(taps_ps, i + 1)
                vec.tensor_tensor(w_taps[:, i, :, :].rearrange("p j c -> p c j"), over(src, TAPS),
                                  taps_bank[i % 2][:, :].rearrange("p (c j) -> p c j", j=TAPS), ALU.mult
                                  ).then_inc(wtap_done, 1)
            dve.wait_ge(lnp_done, 1)
            pre_ab = pre.rearrange("p (n k) -> p n k", k=2 * H)
            lnp_ab = lnp.rearrange("p (n k) -> p n k", k=2 * H)
            g_v = g[:, :].rearrange("p (n h) -> p n h", h=H)
            lnb_v = lnb[:, :].rearrange("p (n h) -> p n h", h=H)
            then_next(vec.scalar_tensor_tensor(out=g_v, in0=pre_ab[:, :, 0:H], scalar=0.0, in1=lnp_ab[:, :, 0:H],
                                               op0=ALU.max, op1=ALU.add))
            dve.wait_ge(ea_done, 1)
            then_next(vec.scalar_tensor_tensor(out=g_v, in0=g_v, scalar=-1.0,
                                               in1=neg_a[:, :].unsqueeze(1).to_broadcast([P, NT, H]),
                                               op0=ALU.mult, op1=ALU.mult))
            then_next(vec.scalar_tensor_tensor(out=lnb_v, in0=pre_ab[:, :, H:2 * H], scalar=0.0,
                                               in1=lnp_ab[:, :, H:2 * H], op0=ALU.min, op1=ALU.subtract
                                               ))
            vec.tensor_scalar(lnb[:, :], lnb[:, :], LN2, None, ALU.add).then_inc(g_done, 1)

            def cum():
                dve.wait_ge(g_done, 1)
                dve.wait_ge(dg_done, 1)
                vec.tensor_tensor(lnb[:, :], lnb[:, :], bank[5][:, 0:P], ALU.subtract).then_inc(lnb_done, 1)

            def logs(s):
                dve.wait_ge(n2_done, 2 * H * (s + 1))
                if s >= 1:
                    dve.wait_ge(norms_done, s)
                    dve.wait_ge(cneg_done, s)
                vec.tensor_scalar(lnn[:, :, :], norm_bank[:, 0:2 * TPG * H].rearrange("p (w n) -> p w n", w=2),
                                  1e-12, None, ALU.max).then_inc(n2_max, 1)
                dve.wait_ge(log_done, s + 1)
                if s >= 1:
                    dve.wait_ge(dmask_done, TPG * s)
                dve.wait_ge(lnb_done, 1)
                vec.tensor_tensor(cneg[:, :], lnb[:, TPG * H * s:TPG * H * (s + 1)], lnn[:, 0, :], ALU.subtract
                                  ).then_inc(cneg_done, 1)

            def vals(s, jj):
                ps = wait_ring(dve, ("vals", s, jj))
                dve.wait_ge(norms_done, s + 1)
                if s >= 1:
                    dve.wait_ge(rhs_done, CPG * s)
                vec.tensor_tensor(nv[:, 2 * jj:2 * jj + 2, :].rearrange("p a (h v) -> p (a h) v", v=VD),
                                             ps[:, :].rearrange("p (h v) -> p h v", v=VD),
                                             over(norm_k[:, 2 * H * jj:2 * H * (jj + 1)], VD), ALU.mult
                                             ).then_inc(nv_done, 1)

            def decay(s, j):
                tile = TPG * s + j
                ps = wait_ring(dve, ("decay", s, j))
                dve.wait_ge(dmask_done, tile + 1)
                vec.tensor_tensor(dec[:, tile % 2], ps[:, :].rearrange("p (h t) -> p h t", t=C),
                                             dec[:, tile % 2], ALU.add).then_inc(darg_done, 1)

            def scores(s, i):
                j, hh = i // 2, i % 2
                tile = TPG * s + j
                hs = slice(HH * hh, HH * hh + HH)
                ps = wait_ring(dve, ("scores", s, i))[:, :].rearrange("p (h w t) -> p h w t", w=2, t=C)
                dve.wait_ge(dec_done, tile + 1)
                if s >= 1:
                    dve.wait_ge(unit_out, 16 * 4 * TPG * s)
                    dve.wait_ge(ring_done, ring_use[("cross1", s - 1, TPG - 1)] + 1)
                    dve.wait_ge(outs_done, CPG * s)
                vec.tensor_tensor(nmat[:, j, hs, :], ps[:, :, 0, :], dec[:, tile % 2, hs, :], ALU.mult)
                vec.tensor_tensor(amat[:, j, hs, :], ps[:, :, 1, :], dec[:, tile % 2, hs, :],
                                             ALU.mult).then_inc(scores_done, 1)

            def invert(s, t):
                base = 63 * s
                if t == 1:
                    dve.wait_ge(unit_in, 16 * (s + 1))
                    vec.memset(unit[:, :, :].rearrange("p i t -> p (i t)")[:, 0:B * B:B + 1], 1.0).then_inc(inv_step, 1)
                dve.wait_ge(inv_step, base + 2 * t - 1)
                cut = prod[:, 0:t * t].rearrange("p (r i) -> p r i", i=t)
                vec.tensor_tensor(cut, unit[:, 0:t, 0:t], unit[:, 0:t, t].unsqueeze(1).to_broadcast([P, t, t]),
                                  ALU.mult).then_inc(inv_step, 1)
                dve.wait_ge(inv_step, base + 2 * t)
                vec.tensor_reduce(unit[:, 0:t, t], cut, AX.X, ALU.add, negate=True).then_inc(inv_step, 1)

            def turn(s, j):
                tile = TPG * s + j
                dve.wait_ge(block_in, 16 * 4 * TPG * (s + 1))
                if tile >= 1:
                    dve.wait_ge(z21_done, tile)
                for a in range(2):
                    rows = slice(C * a, C * a + B)
                    last = vec.transpose(t11[rows], umat[rows, j, :, 0:B])
                last.then_inc(t11_done, 1)

            def keys(s, i):
                j, hh = i // 2, i % 2
                tile = TPG * s + j
                ps = wait_ring(dve, ("keys", s, i))
                dve.wait_ge(dend_done, tile + 1)
                if tile >= 2:
                    dve.wait_ge(state_mm, 2 * (tile - 1))
                vec.tensor_tensor(keyd[:, tile % 2, HH * hh:HH * hh + HH, :],
                                             ps[:, :].rearrange("p (h k) -> p h k", k=P),
                                             over(dend[:, j, HH * hh:HH * hh + HH], P), ALU.mult
                                             ).then_inc(keyd_done, 1)

            def read(s, i):
                c = CPG * s + i
                a, tile = c % 2, c // 2
                rows = slice(C * a, C * a + C)
                dve.wait_ge(read_done, c + 1)
                k_rows = slice(C * (1 - a), C * (2 - a))
                vec.tensor_tensor(heads(gpk[rows, :]), heads(read_ps[k_rows, :]),
                                  over(tile_heads(decay_kq[k_rows, a], tile), VD), ALU.mult).then_inc(gp_step, 1)
                vec.tensor_tensor(heads(gpq[rows, :]), heads(read_ps[rows, :]),
                                  over(tile_heads(decay_kq[rows, a], tile), VD), ALU.mult).then_inc(gp_step, 1)
                dve.wait_ge(gp_step, 2 * c + 1)
                dve.wait_ge(nv_done, TPG // 2 * (s + 1))
                if c >= 2:
                    dve.wait_ge(solve_done, c - 1)
                vec.tensor_tensor(rhs[rows, :], nv[rows, tile % TPG, :], gpk[rows, :], ALU.subtract
                                  ).then_inc(rhs_done, 1)

            def new_state(s, i):
                c = CPG * s + i
                dve.wait_ge(state_mm, c + 1)
                dve.wait_ge(stateg_done, c + 1)
                vec.tensor_tensor(state[:, (c + 1) % 2, :], state_ps, state_g[:, :], ALU.add).then_inc(state_done, 1)

            def outs(s, i):
                c = CPG * s + i
                tile = c // 2
                rows = slice(C * (c % 2), C * (c % 2) + C)
                dve.wait_ge(outs_done, c + 1)
                dve.wait_ge(gp_step, 2 * c + 2)
                if s >= 1:
                    dve.wait_ge(o_ready, tile - TPG + 1)
                    dve.wait_ge(ring_done, ring_use[("mix", s - 1, i // 2)] + 1)
                vec.tensor_tensor(o_t[rows, tile % TPG, :], outs_ps[rows, :], gpq[rows, :], ALU.add
                                  ).then_inc(o_done, 1)

            def rms(s, j):
                tile = TPG * s + j
                o = o_t[:, tile % TPG, :]
                dve.wait_ge(o_done, 2 * tile + 2)
                dve.wait_ge(norms_done, s + 1)
                vec.tensor_tensor(heads(o), heads(o), over(tile_heads(inv_q[s % 2], j), VD), ALU.mult
                                  ).then_inc(rms_step, 1)
                dve.wait_ge(rms_step, 3 * tile + 1)
                vec.tensor_tensor(osq[:, :], o, o, ALU.mult).then_inc(rms_step, 1)
                dve.wait_ge(rms_step, 3 * tile + 2)
                if tile >= 1:
                    dve.wait_ge(rms_done, tile)
                vec.tensor_reduce(oss[:, :], heads(osq[:, :]), AX.X, ALU.add).then_inc(rms_step, 1)
                dve.wait_ge(gate_done, TPG // 2 * (s + 1))
                then_next(vec.tensor_tensor(o, o, gate[s % 2][:, j, :], ALU.mult))
                dve.wait_ge(rms_done, tile + 1)
                vec.tensor_tensor(heads(o), heads(o), over(orms[:, :], VD), ALU.mult).then_inc(o_ready, 1)

            def layer_stats(src, step_sem, base):
                vec.bn_stats(stats[:, :], src).then_inc(step_sem, 1)
                dve.wait_ge(step_sem, base + 2)
                vec.bn_aggr(mv[:, :], stats[:, :]).then_inc(step_sem, 1)

            def mix(s, j):
                tile = TPG * s + j
                ps = wait_ring(dve, ("mix2", s, j))
                dve.wait_ge(xres_in[tile % 2], 16 * (tile // 2 + 1))
                vec.tensor_tensor(x1[:, :], ps[:, 0:P], xres[:, tile % 2, :], ALU.add
                                             ).then_inc(ln_step, 1)
                dve.wait_ge(ln_step, 3 * tile + 1)
                layer_stats(x1[:, :], ln_step, 3 * tile)
                dve.wait_ge(ln_step, 3 * tile + 3)
                dve.wait_ge(rstd_done, tile + 1)
                vec.tensor_scalar(xn[:, j % 2, :], x1[:, :], mv[:, 0:1], rstd[:, 0:1], ALU.subtract, ALU.mult
                                  ).then_inc(xn_done, 1)

            def ln1(s, j):
                tile = TPG * s + j
                ps = wait_ring(dve, ("ln1", s, j))
                dve.wait_ge(xh_done, tile + 1)
                vec.tensor_tensor(xh[:, 1, :], ps[:, 0:P], xh[:, 0, :], ALU.subtract
                                             ).then_inc(xlo_done, 1)

            def hidden(name, s, j, buf):
                ps = wait_ring(dve, (name, s, j))
                dve.wait_ge(h_hi, 2 * (TPG * s + j) + (2 if name == "mid" else 1))
                vec.scalar_tensor_tensor(out=buf[:, 1, :], in0=ps[:, :], scalar=0.0, in1=buf[:, 0, :],
                                                    op0=ALU.max, op1=ALU.subtract).then_inc(h_lo, 1)

            def down(s, j):
                tile = TPG * s + j
                ps = wait_ring(dve, ("down", s, j))
                vec.scalar_tensor_tensor(out=x3[:, :], in0=ps[:, 0:P], scalar=s_work[:, 5:6],
                                                    in1=xn[:, tile % 2, :], op0=ALU.mult, op1=ALU.add
                                                    ).then_inc(y_step, 1)
                dve.wait_ge(y_step, 3 * tile + 1)
                layer_stats(x3[:, :], y_step, 3 * tile)
                dve.wait_ge(y_step, 3 * tile + 3)
                dve.wait_ge(y_rstd, tile + 1)
                if tile >= 2:
                    dve.wait_ge(stored[tile % 2], 16 * (tile // 2))
                vec.tensor_scalar(fin[:, tile % 2, :], x3[:, :], mv[:, 0:1], rstd[:, 0:1], ALU.subtract, ALU.mult
                                  ).then_inc(fin_done, 1)

            do = {"decay": decay, "scores": scores, "invert": invert, "turn": turn, "keys": keys,
                  "read": read, "state": new_state, "outs": outs, "rms": rms, "mix": mix, "ln1": ln1, "down": down,
                  "vals": vals}
            for name, s, i in steps:
                if name == "logs":
                    logs(s)
                elif name == "cum":
                    cum()
                elif name in ("up", "mid"):
                    hidden(name, s, i, h1 if name == "up" else h2)
                elif name in do:
                    do[name](s, i)

        @block.tensor
        def _(pe):
            mm = nc.tensor.matmul
            pe.wait_ge(consts, 1)
            for q in range(4):
                pe.wait_ge(ld_x[q], 16)
                for n in range(4):
                    last = nc.tensor.transpose(bank[q][:, n * P:(n + 1) * P], x_in[:, 4 * q + n, :], ident[:, :])
                last.then_inc(xt_ps, 1)
            pe.wait_ge(ld_small, 16 * N_SMALL + 16)
            for n in range(NT):
                if n % 4 == 0:
                    pe.wait_ge(xt_done, n // 4 + 1)
                last = mm(bank[4][:, n * 2 * H:(n + 1) * 2 * H], xT[:, TAPS - 1 + n * P:TAPS - 1 + (n + 1) * P], wab[:, :],
                          start=True, stop=True)
            last.then_inc(z_ps, 1)
            pe.wait_ge(ld_w, 16 * N_W)
            pe.wait_ge(consts, 2)
            for i in range(NP):
                m, w = i // 2, i % 2
                row = tap_rows[:, w, m * 4 * P:(m + 1) * 4 * P] if m < H else tap_row_v[:, w * 4 * P:(w + 1) * 4 * P]
                if i >= 2:
                    pe.wait_ge(wtap_done, i - 1)
                mm(taps_bank[i % 2][:, :], ones_row, row, start=True, stop=True).then_inc(taps_ps, 1)

            def cum():
                pe.wait_ge(g_done, 1)
                mm(bank[5][:, 0:P], upto, g[:, :], start=True, stop=True)
                for a in range(2):
                    mm(bank[5][:, P * (1 + a):P * (2 + a)], tri_kq[:, a, :, :].rearrange("p w t -> p (w t)"), g[:, :],
                       start=True, stop=True)
                for a in range(2):
                    last = mm(bank[6][:, P * a:P * (1 + a)], in_chunk[:, a, :], g[:, :], start=True, stop=True)
                last.then_inc(cum_ps, 1)

            def take_ring(step):
                n = ring_use[step]
                if n >= 3:
                    pe.wait_ge(*bank_read(ring_steps[n - 3]))
                elif n == 2:
                    pe.wait_ge(dg_done, 1)
                return ring_bank[n % 3]

            def proj(s, i):
                n = NP * s + i
                if n >= 2:
                    pe.wait_ge(silu_done, n - 1)
                if s == 0:
                    pe.wait_ge(wtap_done, i + 1)
                for j in range(TAPS):
                    last = mm(proj_bank[i % 2][:, :], w_taps[:, i, j, :], xT[:, s * GT + j:(s + 1) * GT + j],
                              start=(j == 0), stop=(j == TAPS - 1))
                last.then_inc(proj_done, 1)

            def norm2(s, i):
                n = 2 * H * s + i
                if i == 0 and s > 0:
                    pe.wait_ge(n2_max, s)
                if i == 0 and s == 0:
                    pe.wait_ge(wtap_done, NP)
                pe.wait_ge(sq_done, n + 1)
                m, w = i // 2, i % 2
                for j in range(TPG):
                    col = (w * TPG + j) * H + m
                    last = mm(norm_bank[:, col:col + 1], sq[:, w, j * P:(j + 1) * P], ones[:, 0:1],
                              start=True, stop=True)
                last.then_inc(n2_done, 1)

            def gates(s, jj):
                ps = take_ring(("gate", s, jj))
                for a in range(2):
                    t0 = TAPS - 1 + s * GT + (2 * jj + a) * P
                    last = mm(ps[:, a * HV:(a + 1) * HV], xT[:, t0:t0 + P], wg[:, :], start=True, stop=True)
                last.then_inc(ring_done, 1)

            def vals(s, jj):
                ps = take_ring(("vals", s, jj))
                pe.wait_ge(silu_done, NP * (s + 1))
                for a in range(2):
                    for w in range(2):
                        last = nc.tensor.transpose(ps[:, a * HV + w * P:a * HV + (w + 1) * P],
                                                   vT[:, w, (2 * jj + a) * P:(2 * jj + a + 1) * P], ident[:, :])
                last.then_inc(ring_done, 1)

            def decay(s, j):
                ps = take_ring(("decay", s, j))
                pe.wait_ge(gtri_done, TPG * s + j + 1)
                mm(ps[:, :], same_chunk[:, :], g_tri[:, :, :].rearrange("p h t -> p (h t)"), start=True, stop=True
                   ).then_inc(ring_done, 1)

            def scores(s, i):
                j, hh = i // 2, i % 2
                ps = take_ring(("scores", s, i))
                for h in range(HH):
                    for a in range(2):
                        tile_kq = kq[s % 2][:, HH * hh + h, j, :]
                        k_cols = tile_kq[:, C * (1 + a):C * (2 + a)]
                        q_cols = tile_kq[:, 3 * C * a:3 * C * a + C]
                        dst = ps[a * C:(a + 1) * C, h * 2 * C:(h + 1) * 2 * C]
                        mm(dst[:, 0:C], k_cols, k_cols, start=True, stop=True)
                        last = mm(dst[:, C:2 * C], k_cols, q_cols, start=True, stop=True)
                last.then_inc(ring_done, 1)

            def cross1(s, j):
                ps = take_ring(("cross1", s, j))
                pe.wait_ge(t11_done, TPG * s + j + 1)
                for a in range(2):
                    src, dst = slice(C * a, C * a + B), slice(C * a + B, C * a + C)
                    for h in range(H):
                        last = mm(ps[dst, h * B:(h + 1) * B], nmat[src, j, h, B:C], t11[src, h, :],
                                  start=True, stop=True)
                last.then_inc(ring_done, 1)

            def cross2(s, j):
                ps = take_ring(("cross2", s, j))
                pe.wait_ge(z21_done, TPG * s + j + 1)
                for a in range(2):
                    src, dst = slice(C * a + B, C * a + C), slice(C * a, C * a + B)
                    for h in range(H):
                        last = mm(ps[dst, h * B:(h + 1) * B], z21[src, h, :], umat[src, j, h, B:C],
                                  start=True, stop=True)
                last.then_inc(ring_done, 1)

            def keys(s, i):
                j, hh = i // 2, i % 2
                ps = take_ring(("keys", s, i))
                for h in range(HH):
                    last = nc.tensor.transpose(ps[:, h * P:(h + 1) * P],
                                               kq[s % 2][:, HH * hh + h, j, C:3 * C], ident[:, :])
                last.then_inc(ring_done, 1)

            def read(s, i):
                c = CPG * s + i
                if c > 0:
                    pe.wait_ge(state_done, c)
                for h in range(H):
                    last = mm(read_ps[:, h * VD:(h + 1) * VD], kq[s % 2][:, h, i // 2, i % 2 * P:(i % 2 + 1) * P],
                              state[:, c % 2, h * VD:(h + 1) * VD], start=True, stop=True)
                last.then_inc(read_done, 1)

            def solve(s, i):
                c = CPG * s + i
                rows = slice(C * (c % 2), C * (c % 2) + C)
                pe.wait_ge(rhs_done, c + 1)
                pe.wait_ge(u12_done, c // 2 + 1)
                if c >= 1:
                    pe.wait_ge(o_done, c)
                for h in range(H):
                    last = mm(solve_ps[rows, h * VD:(h + 1) * VD], umat[rows, i // 2, h, :],
                              rhs[rows, h * VD:(h + 1) * VD], start=True, stop=True)
                last.then_inc(solve_done, 1)

            def new_state(s, i):
                c = CPG * s + i
                rows = slice(C * (c % 2), C * (c % 2) + C)
                pe.wait_ge(sol_done, c + 1)
                pe.wait_ge(gp_step, 2 * c + 2)
                pe.wait_ge(keyd_done, 2 * (c // 2) + 2)
                for h in range(H):
                    last = mm(state_ps[:, h * VD:(h + 1) * VD], keyd[rows, c // 2 % 2, h, :],
                              sol[rows, h * VD:(h + 1) * VD], start=True, stop=True)
                last.then_inc(state_mm, 1)

            def outs(s, i):
                c = CPG * s + i
                rows = slice(C * (c % 2), C * (c % 2) + C)
                for h in range(H):
                    last = mm(outs_ps[rows, h * VD:(h + 1) * VD], amat[rows, i // 2, h, :],
                              sol[rows, h * VD:(h + 1) * VD], start=True, stop=True)
                last.then_inc(outs_done, 1)

            def mix(s, j):
                tile = TPG * s + j
                ps = take_ring(("mix", s, j))
                pe.wait_ge(o_ready, tile + 1)
                for w in range(2):
                    last = nc.tensor.transpose(ps[:, w * P:(w + 1) * P], o_t[:, tile % TPG, w * P:(w + 1) * P], ident[:, :])
                last.then_inc(ring_done, 1)
                ps = take_ring(("mix2", s, j))
                pe.wait_ge(ot_done, tile + 1)
                for w in range(2):
                    last = mm(ps[:, 0:P], oT[:, w, :], wo[:, w, :], start=(w == 0), stop=(w == 1))
                last.then_inc(ring_done, 1)

            def ln1(s, j):
                ps = take_ring(("ln1", s, j))
                pe.wait_ge(xn_done, TPG * s + j + 1)
                nc.tensor.transpose(ps[:, 0:P], xn[:, j % 2, :], ident[:, :]).then_inc(ring_done, 1)

            def up(s, j):
                ps = take_ring(("up", s, j))
                pe.wait_ge(xlo_done, TPG * s + j + 1)
                pe.wait_ge(mlpw_done, 1)
                for f in range(4):
                    cols = slice(f * P, (f + 1) * P)
                    for part in range(2):
                        last = mm(ps[:, cols], w0[:, cols], xh[:, part, :], start=(part == 0), stop=(part == 1))
                last.then_inc(ring_done, 1)

            def mid(s, j):
                ps = take_ring(("mid", s, j))
                pe.wait_ge(h_lo, 2 * (TPG * s + j) + 1)
                for f in range(4):
                    cols = slice(f * P, (f + 1) * P)
                    for k in range(4):
                        for part in range(2):
                            last = mm(ps[:, cols], w1[:, k, cols], h1[:, part, k * P:(k + 1) * P],
                                      start=(k == 0 and part == 0), stop=(k == 3 and part == 1))
                last.then_inc(ring_done, 1)

            def down(s, j):
                ps = take_ring(("down", s, j))
                pe.wait_ge(h_lo, 2 * (TPG * s + j) + 2)
                for k in range(4):
                    for part in range(2):
                        last = mm(ps[:, 0:P], h2[:, part, k * P:(k + 1) * P], w2[:, k, :],
                                  start=(k == 0 and part == 0), stop=(k == 3 and part == 1))
                last.then_inc(ring_done, 1)

            do = {"proj": proj, "norm2": norm2, "gate": gates, "vals": vals, "decay": decay, "scores": scores,
                  "cross1": cross1, "cross2": cross2, "keys": keys, "read": read, "solve": solve,
                  "state": new_state, "outs": outs, "mix": mix, "ln1": ln1, "up": up, "mid": mid, "down": down}
            for name, s, i in steps:
                if name == "cum":
                    cum()
                elif name in do:
                    do[name](s, i)


_NAMES = ("L0_attn_x L0_attn_Wq L0_attn_Wk L0_attn_Wv L0_attn_Wa L0_attn_Wb L0_attn_Wg L0_attn_Wo L0_attn_A_log "
          "L0_attn_dt_bias L0_attn_conv_q L0_attn_conv_k L0_attn_conv_v L0_attn_o_norm_w L0_ffn_k0 L0_ffn_k1 "
          "L0_ffn_k2 L0_ffn_s0 L0_ffn_s1 L0_ffn_s2").split()


def kernel(**inputs):
    import numpy as np
    import concourse.bacc as bacc
    from concourse.bass_utils import run_bass_kernel_spmd

    nc = bacc.Bacc("TRN2", target_bir_lowering=False, num_devices=1)
    arrays, args = {}, []
    for name in _NAMES:
        a = np.ascontiguousarray(inputs[name])
        if name == "L0_attn_x":
            a = a.reshape(a.shape[1:])
        if a.ndim == 0:
            a = a.reshape(1)
        arrays[f"in_{name}"] = a
        args.append(nc.dram_tensor(f"in_{name}", a.shape, mybir.dt.from_np(a.dtype), kind="ExternalInput").ap())
    T, D = arrays["in_L0_attn_x"].shape
    args.append(nc.dram_tensor("out", (T, D), F32, kind="ExternalOutput").ap())
    post_ln_block(nc, *args)
    r = run_bass_kernel_spmd(nc, [arrays], core_ids=[0])
    return r.results[0]["out"].reshape(1, T, D)
```

```python
from contextlib import ExitStack

import concourse.bass as bass
from concourse import mybir

F32 = mybir.dt.float32
F16 = mybir.dt.float16
U8 = mybir.dt.uint8
ALU = mybir.AluOpType
ACT = mybir.ActivationFunctionType
AX = mybir.AxisListType

P = 128
C = 64
B = 32
GT = 512
TPG = GT // P
CPG = GT // C
TAPS = 4
EPS = 1e-5
NEG = -1e30
EARLY = 20
LN_EXP = "natural_log_exp_and_others"
LN2 = 0.6931471805599453


def weave(a, b):
    at = sorted([((k + 0.5) / len(a), 0, k) for k in range(len(a))] + [((k + 0.5) / len(b), 1, k) for k in range(len(b))])
    return [(a, b)[which][k] for _, which, k in at]


def order(groups, heads):
    def project(s):
        if s >= groups:
            return []
        out = []
        for i in range(2 * heads):
            out += [("begin", s, i), ("proj", s, i)]
            if i >= 2:
                out.append(("norm2", s, i - 2))
        out += [("norm2", s, i) for i in (2 * heads - 2, 2 * heads - 1)]
        out += [(name, s, i) for i in (2 * heads, 2 * heads + 1) for name in ("begin", "proj")]
        return out + [("gate", s, jj) for jj in range(TPG // 2)]

    def prepare(s):
        if s >= groups:
            return []
        first = [("logs", s, 0)] + [("vals", s, jj) for jj in range(TPG // 2)]
        blocks = []
        for j in range(TPG):
            blocks.append(("decay", s, j))
            for hh in range(2):
                blocks.append(("scores", s, 2 * j + hh))
        blocks.append(("units", s, 0))
        if s > 0:
            blocks = weave(blocks, finish(s - 1, TPG - 1))
        invert = [("invert", s, t) for t in range(1, B)] + [("blocks", s, 0)]
        return first + blocks + weave(invert, project(s + 1)[:EARLY])

    def recur(s, j):
        c = 2 * j
        out = [("keys", s, c), ("keys", s, c + 1), ("read_half", s, c), ("read", s, c)]
        if j == 0:
            out += [("turn", s, 0), ("cross1", s, 0), ("cross2", s, 0)]
        out += [("solve", s, c), ("state_half", s, c), ("state", s, c), ("outs", s, c)]
        if j + 1 < TPG:
            out += [("turn", s, j + 1), ("cross1", s, j + 1)]
        out += [("read_half", s, c + 1), ("read", s, c + 1)]
        if j + 1 < TPG:
            out.append(("cross2", s, j + 1))
        return out + [("solve", s, c + 1), ("state_half", s, c + 1), ("state", s, c + 1), ("outs", s, c + 1)]

    def finish(s, j):
        return [(name, s, j) for name in ("rms", "gated", "turn_o", "mix", "ln1", "split", "up", "mid", "down", "ln2")]

    steps = project(0) + [("cum", 0, 0)] + prepare(0)
    for s in range(groups):
        ahead = project(s + 1)[EARLY:]
        n = -(-len(ahead) // TPG)
        for j in range(TPG):
            part = weave(ahead[j * n:(j + 1) * n], finish(s, j - 1) if j else [])
            steps += weave(recur(s, j), part)
        steps += prepare(s + 1)
    return steps + finish(groups - 1, TPG - 1)


def post_ln_block(nc, x, Wq, Wk, Wv, Wa, Wb, Wg, Wo, A_log, dt_bias, conv_q, conv_k, conv_v, o_norm_w,
                  k0, k1, k2, s0, s1, s2, out):
    T, D = x.shape
    H = A_log.shape[0]
    VD = Wv.shape[1] // H
    HV = H * VD
    F = k1.shape[0]
    assert D == P and Wq.shape[1] == H * P and HV == 2 * P and F == 4 * P and T % GT == 0
    NT = T // P
    NG = T // GT
    NP = 2 * H + 2
    HH = H // 2

    steps = order(NG, H)
    ring_use = {}
    for st in steps:
        name, s, i = st
        if name in ("logs", "gate", "vals", "decay", "scores", "cross1", "cross2", "keys", "turn_o", "mix", "split", "up", "mid", "down"):
            ring_use[st] = len(ring_use)
    ring_steps = list(ring_use)

    with ExitStack() as ctx:
        def sb(name, shape, dt=F32):
            return ctx.enter_context(nc.sbuf_tensor(name, shape, dt))

        def sem(name):
            return ctx.enter_context(nc.semaphore(name))

        bank = [ctx.enter_context(nc.psum_tensor(f"bank{i}", [P, 512], F32)) for i in range(8)]
        proj_bank, ring_bank, norm_bank = bank[0:2], (bank[2], bank[3], bank[6]), bank[7]
        read_ps = bank[4][:, 0:HV]
        state_ps = bank[4][:, HV:2 * HV]
        solve_ps = bank[5][:, 0:HV]
        outs_ps = bank[5][:, HV:2 * HV]

        ident = sb("ident", [P, P])
        pick = sb("pick", [P, 4 * H - 1])
        eps = sb("eps", [P, 1])
        same_chunk = sb("same_chunk", [P, P])
        tri = sb("tri", [P, C])
        later = sb("later", [P, C])
        w_taps = sb("w_taps", [P, NP, TAPS, P])
        wg = sb("wg", [P, HV])
        wab = sb("wab", [P, 2 * H])
        wo = sb("wo", [P, 2, P])
        bias_ab = sb("bias_ab", [P, 2 * H])
        neg_a = sb("neg_a", [P, H])
        onw = sb("onw", [P, VD])
        s_in = sb("s_in", [P, 3])
        s_work = sb("s_work", [P, 6])
        w0 = sb("w0", [P, F], F16)
        w1 = sb("w1", [P, 4, F], F16)
        w2 = sb("w2", [P, 4, P], F16)

        xT = sb("xT", [P, TAPS - 1 + T])
        g = sb("g", [P, NT * H])
        lnb = sb("lnb", [P, NT * H])
        decay_kq = sb("decay_kq", [P, 2, NT * H])
        decay_end = sb("decay_end", [P, 2, NT * H])

        kq = [sb(f"kq{i}", [P, H, TPG, 4 * C]) for i in range(2)]
        sq = sb("sq", [P, 2, GT])
        vT = sq
        lnn = sb("lnn", [P, 2, TPG * H])
        norm_k = sb("norm_k", [P, TPG * H])
        inv_q = [sb(f"inv_q{i}", [P, TPG * H]) for i in range(2)]
        cneg = sb("cneg", [P, TPG * H])
        g_tri = sb("g_tri", [P, H, C])
        dec = sb("dec", [P, 2, H, C])
        dend = sb("dend", [P, TPG, H])
        nmat = sb("nmat", [P, TPG, H, C])
        amat = sb("amat", [P, TPG, H, C])
        unit = sb("unit", [P, B, B])
        prod = sb("prod", [P, B * B])
        umat = sb("umat", [P, TPG, H, C])
        t11 = sb("t11", [P, H, B])
        z21 = sb("z21", [P, H, B])
        nv = sb("nv", [P, TPG, HV])
        gate = [sb(f"gate{i}", [P, TPG, HV]) for i in range(2)]
        keyd = sb("keyd", [P, 2, H, P])
        state = sb("state", [P, 2, HV])
        state_g = sb("state_g", [P, HV])
        gpk = sb("gpk", [P, HV])
        gpq = sb("gpq", [P, HV])
        rhs = sb("rhs", [P, HV])
        sol = sb("sol", [P, HV])
        o_t = sb("o_t", [P, TPG, HV])
        osq = gpk
        oss = sb("oss", [P, H])
        orms = sb("orms", [P, H])
        oT = sb("oT", [P, 2, P])
        xres = sb("xres", [P, 2, P])
        x1 = sb("x1", [P, P])
        stats = sb("stats", [P, 6])
        mv = sb("mv", [P, 2])
        rstd = sb("rstd", [P, 1])
        xn = sb("xn", [P, 2, P])
        xh = sb("xh", [P, 2, P], F16)
        h1 = sb("h1", [P, 2, F], F16)
        h2 = sb("h2", [P, 2, F], F16)
        x3 = x1
        fin = sb("fin", [P, 2, P])

        x_in = nmat[:, :, :, :].rearrange("p a h t -> p (a h t)").rearrange("p (n d) -> p n d", d=P)
        upto = keyd[:, 0, 0, :]
        in_chunk = keyd[:, 0, 1:3, :]
        tri_kq = keyd[:, 0, 3:5, :].rearrange("p a (w t) -> p a w t", w=2)
        n2_rows = prod[0:2 * H, 0:GT]
        wqk_raw = umat[:, :, :, :].rearrange("p n h t -> p (n h t)").rearrange("p (w d) -> p w d", w=2)
        wv_raw = t11[:, :, :].rearrange("p h t -> p (h t)")
        taps_qk = kq[1][:, :, :, :].rearrange("p h n t -> p (h n t)").rearrange("p (w d) -> p w d", w=2)
        taps_v = prod[:, :]
        k_raw = unit[:, :, :].rearrange("p i t -> p (i t)").bitcast(U8)
        k0_raw = k_raw[:, 0:2 * F].rearrange("p (a f) -> p a f", a=2)
        k1_raw = k_raw[:, 2 * F:6 * F].rearrange("p (a f) -> p a f", a=4)
        k2_raw = k_raw[:, 6 * F:6 * F + 4 * P].rearrange("p (a f) -> p a f", a=4)
        pre = amat[:, 0, :, :].rearrange("p h t -> p (h t)")[:, 0:2 * NT * H]
        mag = amat[:, 1, :, :].rearrange("p h t -> p (h t)")[:, 0:2 * NT * H]
        lnp = amat[:, 2, :, :].rearrange("p h t -> p (h t)")[:, 0:2 * NT * H]
        w0_raw = amat[:, 3, :, :].rearrange("p h t -> p (h t)").bitcast(F16).rearrange("p (a f) -> p a f", a=2)

        scratch = nc.dram_tensor("scratch", (2, 2, P, B * B), F32, kind="Internal").ap()

        ld_x = [sem(f"ld_x{q}") for q in range(4)]
        ld_taps = [sem(f"ld_taps{q}") for q in range(5)]
        ld_w, ld_small, ld_mlp = sem("ld_w"), sem("ld_small"), sem("ld_mlp")
        consts = sem("consts")
        pool_done = sem("pool_done")
        dve_done = sem("dve_done")
        act_done = sem("act_done")
        xt_ps, xt_done = sem("xt_ps"), sem("xt_done")
        z_ps, cum_ps = sem("z_ps"), sem("cum_ps")
        mag_done, lnp_done, g_done, lnb_done, dg_done = (sem("mag_done"), sem("lnp_done"), sem("g_done"),
                                                         sem("lnb_done"), sem("dg_done"))
        ea_done, mlpw_step, mlpw_done, sgn_done = sem("ea_done"), sem("mlpw_step"), sem("mlpw_done"), sem("sgn_done")
        proj_done, wtap_done = sem("proj_done"), sem("wtap_done")
        silu_done, sq_done, n2_done = sem("silu_done"), sem("sq_done"), sem("n2_done")
        ring_done = sem("ring_done")
        rows_done = sem("rows_done")
        n2_max, log_done, norms_done, cneg_done = sem("n2_max"), sem("log_done"), sem("norms_done"), sem("cneg_done")
        gate_act, gate_done = sem("gate_act"), sem("gate_done")
        gtri_done, dmask_done, darg_done, dec_done, dend_done = (sem("gtri_done"), sem("dmask_done"),
                                                                 sem("darg_done"), sem("dec_done"), sem("dend_done"))
        scores_done = sem("scores_done")
        unit_out, unit_in = sem("unit_out"), sem("unit_in")
        block_out = [sem(f"block_out{j}") for j in range(TPG)]
        block_in = [sem(f"block_in{j}") for j in range(TPG)]
        inv_step = sem("inv_step")
        t11_done, z21_done, u12_done, nv_done = sem("t11_done"), sem("z21_done"), sem("u12_done"), sem("nv_done")
        zero_done = sem("zero_done")
        keyd_done = sem("keyd_done")
        read_done, gp_step, rhs_done = sem("read_done"), sem("gp_step"), sem("rhs_done")
        solve_done, sol_done, state_mm, state_done, stateg_done = (sem("solve_done"), sem("sol_done"),
                                                                   sem("state_mm"), sem("state_done"),
                                                                   sem("stateg_done"))
        outs_done, o_done = sem("outs_done"), sem("o_done")
        rms_step, rms_ln, rms_done, o_ready = sem("rms_step"), sem("rms_ln"), sem("rms_done"), sem("o_ready")
        ot_done, ln_step, ln_ln, rstd_done, xn_done = (sem("ot_done"), sem("ln_step"),
                                                                sem("ln_ln"), sem("rstd_done"), sem("xn_done"))
        xh_done, xlo_done, h_hi, h_lo = sem("xh_done"), sem("xlo_done"), sem("h_hi"), sem("h_lo")
        y_step, y_ln, y_rstd, fin_done = sem("y_step"), sem("y_ln"), sem("y_rstd"), sem("fin_done")
        xres_in = [sem(f"xres_in{i}") for i in range(2)]
        stored = [sem(f"stored{i}") for i in range(2)]

        NCONST = 12
        N_SMALL, N_W, N_MLP = 9, 3, 3

        def tile_heads(ap, tile):
            return ap[:, tile * H:(tile + 1) * H]

        def keys_of(buf, h):
            return buf[:, h, :, C:3 * C]

        def queries_of(buf, h):
            return buf[:, h, :, :].rearrange("p n (a t) -> p n a t", a=4)[:, :, 0:4:3, :]

        def over(ap, n):
            return ap.unsqueeze(len(ap.shape)).to_broadcast(list(ap.shape) + [n])

        def heads(ap):
            return ap.rearrange("p (h v) -> p h v", v=VD)

        def wait_ring(eng, step):
            eng.wait_ge(ring_done, ring_use[step] + 1)
            return ring_bank[ring_use[step] % 3]

        def bank_read(step):
            name, s, i = step
            tile = TPG * s + i
            return {"logs": (n2_max, s + 1), "gate": (gate_act, TPG // 2 * s + i + 1),
                    "vals": (nv_done, TPG // 2 * s + i + 1), "decay": (darg_done, tile + 1),
                    "scores": (scores_done, 2 * TPG * s + i + 1), "keys": (keyd_done, 2 * TPG * s + i + 1),
                    "cross1": (z21_done, tile + 1), "cross2": (u12_done, tile + 1),
                    "turn_o": (ot_done, tile + 1), "mix": (ln_step, 3 * tile + 1), "split": (xlo_done, tile + 1),
                    "up": (h_lo, 2 * tile + 1), "mid": (h_lo, 2 * tile + 2), "down": (y_step, 3 * tile + 1)}[name]

        block = ctx.enter_context(nc.Block())

        @block.sync
        def _(sp):
            for q in range(4):
                sp.dma_start(x_in[:, 4 * q:4 * q + 4, :],
                             x[4 * q * P:(4 * q + 4) * P, :].rearrange("(n p) d -> p n d", p=P)).then_inc(ld_x[q], 16)
            sp.dma_start(wab[:, 0:H], Wa).then_inc(ld_small, 16)
            sp.dma_start(wab[:, H:2 * H], Wb).then_inc(ld_small, 16)
            sp.dma_start(bias_ab[:, 0:H], dt_bias.partition_broadcast(P)).then_inc(ld_small, 16)
            sp.dma_start(neg_a[:, :], A_log.partition_broadcast(P)).then_inc(ld_small, 16)
            sp.dma_start(onw[:, :], o_norm_w.partition_broadcast(P)).then_inc(ld_small, 16)
            sp.dma_start(wg[:, :], Wg).then_inc(ld_small, 16)
            sp.dma_start(wo[:, :, :], Wo.rearrange("(a p) n -> p a n", p=P)).then_inc(ld_small, 16)
            for n, s_n in enumerate((s0, s1, s2)):
                sp.dma_start(s_in[:, n:n + 1], s_n.partition_broadcast(P)).then_inc(ld_small, 16)
            sp.dma_start(wqk_raw[:, 0, :], Wk).then_inc(ld_w, 16)
            sp.dma_start(wqk_raw[:, 1, :], Wq).then_inc(ld_w, 16)
            sp.dma_start(wv_raw, Wv).then_inc(ld_w, 16)
            n = HH * P * TAPS
            for half in range(2):
                for w, conv in enumerate((conv_k, conv_q)):
                    sp.dma_start(taps_qk[:, w, half * n:(half + 1) * n],
                                 conv.rearrange("c j -> (c j)")[half * n:(half + 1) * n].partition_broadcast(P)
                                 ).then_inc(ld_taps[2 * half + w], 16)
            sp.dma_start(taps_v, conv_v.rearrange("c j -> (c j)").partition_broadcast(P)).then_inc(ld_taps[4], 16)
            sp.dma_start(k0_raw, k0.rearrange("(a p) f -> p a f", p=P)).then_inc(ld_mlp, 16)
            sp.dma_start(k1_raw, k1.rearrange("(a p) f -> p a f", p=P)).then_inc(ld_mlp, 16)
            sp.dma_start(k2_raw, k2.rearrange("(a p) f -> p a f", p=P)).then_inc(ld_mlp, 16)

            def to_units(s, j):
                sp.wait_ge(scores_done, 2 * (TPG * s + j) + 2)
                for b in range(4):
                    u = (4 * j + b) * H
                    sp.dma_start(scratch[0, s % 2, u:u + H, :].rearrange("h (i t) -> i h t", t=B),
                                 nmat[b * B:(b + 1) * B, j, :, b % 2 * B:(b % 2 + 1) * B]).then_inc(unit_out, 16)

            for name, s, i in steps:
                if name == "scores" and i % 2:
                    to_units(s, i // 2)
                elif name == "units":
                    sp.wait_ge(unit_out, 16 * 4 * TPG * (s + 1))
                    if s == 0:
                        sp.wait_ge(mlpw_done, 2)
                    else:
                        for j in range(TPG):
                            sp.wait_ge(block_out[j], 16 * s)
                    sp.dma_start(unit[:, :, :].rearrange("p i t -> p (i t)"), scratch[0, s % 2]).then_inc(unit_in, 16)
                elif name == "blocks":
                    sp.wait_ge(inv_step, 63 * (s + 1))
                    for j in range(TPG):
                        us = slice(4 * H * j, 4 * H * (j + 1))
                        sp.dma_start(scratch[1, s % 2, us], unit[us, :, :].rearrange("p i t -> p (i t)")
                                     ).then_inc(block_out[j], 16)
                    if s >= 1:
                        sp.wait_ge(solve_done, CPG * s)
                    sp.wait_ge(zero_done, 1)
                    for j in range(TPG):
                        sp.wait_ge(block_out[j], 16 * (s + 1))
                        for b in range(4):
                            u = (4 * j + b) * H
                            sp.dma_start(umat[b * B:(b + 1) * B, j, :, b % 2 * B:(b % 2 + 1) * B],
                                         scratch[1, s % 2, u:u + H, :].rearrange("h (i t) -> i h t", t=B)
                                         ).then_inc(block_in[j], 16)
                elif name == "rms":
                    tile = TPG * s + i
                    if tile >= 2:
                        sp.wait_ge(ln_step, 3 * (tile - 2) + 1)
                    sp.dma_start(xres[:, tile % 2, :], x[tile * P:(tile + 1) * P, :]).then_inc(xres_in[tile % 2], 16)
                elif name == "ln2":
                    tile = TPG * s + i
                    sp.wait_ge(fin_done, tile + 1)
                    sp.dma_start(out[tile * P:(tile + 1) * P, :], fin[:, tile % 2, :]).then_inc(stored[tile % 2], 16)
            for i in range(2):
                sp.wait_ge(stored[i], 16 * NT // 2)
            sp.wait_ge(unit_out, 16 * 4 * TPG * NG)
            for j in range(TPG):
                sp.wait_ge(block_out[j], 16 * NG)

        @block.gpsimd
        def _(pool):
            n_done = [0]

            def then_next(ins):
                n_done[0] += 1
                ins.then_inc(pool_done, 1)
                pool.wait_ge(pool_done, n_done[0])

            nc.gpsimd.memset(pick[:, :], 0.0)
            nc.gpsimd.memset(eps[:, :], EPS)
            nc.gpsimd.memset(xT[:, 0:TAPS - 1], 0.0)
            nc.gpsimd.memset(bias_ab[:, H:2 * H], 0.0)
            nc.gpsimd.memset(state[:, 0, :], 0.0)
            nc.gpsimd.memset(later[:, :], 0.0)
            nc.gpsimd.memset(tri[:, :], 1.0)
            nc.gpsimd.memset(same_chunk[:, :], 0.0)
            nc.gpsimd.memset(tri_kq, 0.0)
            nc.gpsimd.memset(in_chunk, 0.0)
            then_next(nc.gpsimd.memset(ident[:, :], 0.0))
            nc.gpsimd.memset(pick[:, 2 * H - 1:2 * H], 1.0)
            nc.gpsimd.affine_select(out=ident[:, :], in_=ident[:, :], compare_op=ALU.not_equal, fill=1.0, base=0,
                                    pattern=[[-1, P]], channel_multiplier=1).then_inc(consts, 1)
            for a in range(2):
                half = slice(C * a, C * a + C)
                nc.gpsimd.memset(same_chunk[half, half], 1.0)
                nc.gpsimd.memset(in_chunk[half, a, :], 1.0)
                nc.gpsimd.affine_select(out=tri[half, :], in_=tri[half, :], compare_op=ALU.is_ge, fill=0.0, base=0,
                                        pattern=[[1, C]], channel_multiplier=-1)
                then_next(nc.gpsimd.affine_select(out=later[half, :], in_=later[half, :], compare_op=ALU.is_ge,
                                                  fill=NEG, base=0, pattern=[[1, C]], channel_multiplier=-1))
            then_next(nc.gpsimd.affine_select(out=upto, in_=same_chunk[:, :], compare_op=ALU.is_ge, fill=0.0, base=0,
                                              pattern=[[1, P]], channel_multiplier=-1))
            for a in range(2):
                half = slice(C * a, C * a + C)
                for w in range(2):
                    last = nc.gpsimd.tensor_copy(tri_kq[half, a, w, :], tri[half, :])
                if a == 0:
                    then_next(last)
            last.then_inc(consts, 1)
            pool.wait_ge(consts, 2)
            pool.wait_ge(wtap_done, NP)
            nc.gpsimd.memset(umat[:, :, :, :], 0.0).then_inc(zero_done, 1)

            def mlp_weights(part):
                if part == 0:
                    pool.wait_ge(ld_mlp, 16 * N_MLP)
                    pool.wait_ge(sgn_done, 1)
                    nc.gpsimd.tensor_scalar(w0_raw, k0_raw, 2.0, None, ALU.mult).then_inc(mlpw_step, 1)
                elif part == 1:
                    pool.wait_ge(mlpw_step, 1)
                    nc.gpsimd.tensor_tensor(w0[:, :], w0_raw[:, 0, :], w0_raw[:, 1, :], ALU.subtract
                                            ).then_inc(mlpw_step, 1)
                elif part == 2:
                    pool.wait_ge(mlpw_step, 2)
                    nc.gpsimd.tensor_scalar(w0[:, :], w0[:, :], s_work[:, 1:2], None, ALU.mult)
                    nc.gpsimd.tensor_scalar(w2[:, :, :], k2_raw, 2.0, -1.0, ALU.mult, ALU.add)
                elif part < 5:
                    ks = slice(2 * (part - 3), 2 * (part - 2))
                    nc.gpsimd.tensor_scalar(w1[:, ks, :], k1_raw[:, ks, :], 2.0, -1.0, ALU.mult, ALU.add
                                            ).then_inc(mlpw_step, 1)
                elif part < 7:
                    ks = slice(2 * (part - 5), 2 * (part - 4))
                    pool.wait_ge(mlpw_step, part - 2)
                    nc.gpsimd.tensor_scalar(w1[:, ks, :], w1[:, ks, :], s_work[:, 3:4], None, ALU.mult
                                            ).then_inc(mlpw_done, 1)

            def squares(s, i):
                if i >= 2 * H:
                    return
                m, w = i // 2, i % 2
                pool.wait_ge(silu_done, NP * s + i + 1)
                if i >= 2:
                    pool.wait_ge(n2_done, 2 * H * s + i - 1)
                elif s > 0:
                    pool.wait_ge(ring_done, ring_use[("vals", s - 1, 1)] + 1)
                if w == 0:
                    src, dst = keys_of(kq[s % 2], m), sq[:, w, :].rearrange("p (n t) -> p n t", t=P)
                else:
                    src, dst = queries_of(kq[s % 2], m), sq[:, w, :].rearrange("p (n a t) -> p n a t", a=2, t=C)
                nc.gpsimd.tensor_tensor(dst, src, src, ALU.mult).then_inc(sq_done, 1)

            def gates(s, jj):
                pool.wait_ge(gate_act, TPG // 2 * s + jj + 1)
                both = gate[s % 2][:, 2 * jj:2 * jj + 2, :].rearrange("p a (h v) -> p (a h) v", v=VD)
                nc.gpsimd.tensor_tensor(both, both, onw[:, :].unsqueeze(1).to_broadcast([P, 2 * H, VD]), ALU.mult
                                        ).then_inc(gate_done, 1)

            def decay(s, j):
                tile = TPG * s + j
                if tile >= 1:
                    pool.wait_ge(darg_done, tile)
                pool.wait_ge(g_done, 1)
                nc.gpsimd.tensor_tensor(g_tri[:, :, :], over(tile_heads(g, tile), C),
                                        tri[:, :].unsqueeze(1).to_broadcast([P, H, C]), ALU.mult
                                        ).then_inc(gtri_done, 1)
                pool.wait_ge(cneg_done, s + 1)
                if tile >= 2:
                    pool.wait_ge(scores_done, 2 * (tile - 1))
                    pool.wait_ge(dend_done, tile - 1)
                nc.gpsimd.tensor_tensor(dec[:, tile % 2], over(tile_heads(cneg, j), C),
                                        later[:, :].unsqueeze(1).to_broadcast([P, H, C]), ALU.add
                                        ).then_inc(dmask_done, 1)

            def stateg(c):
                if c > 0:
                    pool.wait_ge(state_done, c)
                nc.gpsimd.tensor_tensor(heads(state_g[:, :]), heads(state[:, c % 2, :]),
                                        over(tile_heads(decay_end[:, c % 2], c // 2), VD), ALU.mult
                                        ).then_inc(stateg_done, 1)

            for name, s, i in steps:
                if name == "proj":
                    squares(s, i)
                    if s == 0 and i % 2 and i >= 3:
                        mlp_weights((i - 3) // 2)
                elif name == "gate":
                    gates(s, i)
                elif name == "decay":
                    decay(s, i)
                elif name == "read":
                    stateg(CPG * s + i)

        @block.scalar
        def _(act):
            nc.scalar.preload_act_table_set(LN_EXP)
            for q in range(4):
                act.wait_ge(xt_ps, q + 1)
                nc.scalar.activation(xT[:, TAPS - 1 + 512 * q:TAPS - 1 + 512 * q + 512], bank[q][:, :], ACT.Copy).then_inc(xt_done, 1)
            act.wait_ge(ld_small, 16 * N_SMALL + 16)
            nc.scalar.activation(neg_a[:, :], neg_a[:, :], ACT.Exp).then_inc(ea_done, 1)
            act.wait_ge(mag_done, 1)
            nc.scalar.activation(mag, mag, ACT.Exp).then_inc(mag_done, 1)
            act.wait_ge(mag_done, 2)
            nc.scalar.activation(lnp, mag, ACT.Ln, bias=1.0).then_inc(lnp_done, 1)
            def cum():
                act.wait_ge(cum_ps, 1)
                nc.scalar.preload_act_table_set(LN_EXP)
                nc.scalar.activation(decay_kq[:, :, :], bank[5][:, P:3 * P].rearrange("p (a n) -> p a n", a=2), ACT.Exp)
                nc.scalar.activation(decay_end[:, :, :], bank[6][:, 0:2 * P].rearrange("p (a n) -> p a n", a=2),
                                     ACT.Exp).then_inc(dg_done, 1)

            def proj(s, i):
                n = NP * s + i
                m, w = i // 2, i % 2
                act.wait_ge(proj_done, n + 1)
                ps = proj_bank[w][:, :]
                if m == H:
                    act.wait_ge(n2_done, 2 * H * s + 2 * H - 1 + w)
                    nc.scalar.activation(vT[:, w, :], ps, ACT.Silu).then_inc(silu_done, 1)
                    return
                if s >= 2:
                    act.wait_ge(read_done, CPG * (s - 1))
                elif s == 1:
                    act.wait_ge(wtap_done, NP)
                if w == 0:
                    nc.scalar.activation(keys_of(kq[s % 2], m), ps.rearrange("p (n t) -> p n t", t=P), ACT.Silu
                                         ).then_inc(silu_done, 1)
                else:
                    nc.scalar.activation(queries_of(kq[s % 2], m), ps.rearrange("p (n a t) -> p n a t", a=2, t=C),
                                         ACT.Silu).then_inc(silu_done, 1)

            def gates(s, jj):
                ps = wait_ring(act, ("gate", s, jj))
                if s >= 2:
                    act.wait_ge(o_ready, TPG * (s - 1))
                nc.scalar.activation(gate[s % 2][:, 2 * jj:2 * jj + 2, :],
                                                ps[:, :].rearrange("p (a n) -> p a n", a=2), ACT.Silu
                                                ).then_inc(gate_act, 1)

            def logs(s):
                nc.scalar.preload_act_table_set(LN_EXP)
                act.wait_ge(n2_max, s + 1)
                if s >= 1:
                    act.wait_ge(cneg_done, s)
                nc.scalar.activation(lnn[:, :, :], lnn[:, :, :], ACT.Ln).then_inc(log_done, 1)
                act.wait_ge(log_done, s + 1)
                if s >= 1:
                    act.wait_ge(nv_done, TPG // 2 * s)
                if s >= 2:
                    act.wait_ge(rms_step, 3 * TPG * (s - 1))
                nc.scalar.activation(norm_k[:, :], lnn[:, 0, :], ACT.Exp, scale=0.5)
                nc.scalar.activation(inv_q[s % 2][:, :], lnn[:, 1, :], ACT.Exp, scale=-0.5).then_inc(norms_done, 1)

            def decay(s, j):
                tile = TPG * s + j
                act.wait_ge(darg_done, tile + 1)
                nc.scalar.activation(dec[:, tile % 2], dec[:, tile % 2], ACT.Exp).then_inc(dec_done, 1)
                act.wait_ge(dec_done, tile + 1)
                if s >= 1:
                    act.wait_ge(keyd_done, 2 * TPG * s)
                nc.scalar.activation(dend[:, j, :], dec[:, tile % 2, :, C - 1], ACT.Copy).then_inc(dend_done, 1)

            def cross1(s, j):
                tile = TPG * s + j
                ps = wait_ring(act, ("cross1", s, j))
                if tile >= 1:
                    act.wait_ge(ring_done, ring_use[("cross2", (tile - 1) // TPG, (tile - 1) % TPG)] + 1)
                for a in range(2):
                    rows = slice(C * a + B, C * a + C)
                    last = nc.scalar.activation(z21[rows], ps[rows, 0:HV].rearrange("p (h t) -> p h t", t=B), ACT.Copy)
                last.then_inc(z21_done, 1)

            def cross2(s, j):
                ps = wait_ring(act, ("cross2", s, j))
                for a in range(2):
                    rows = slice(C * a, C * a + B)
                    last = nc.scalar.activation(umat[rows, j, :, B:C],
                                                ps[rows, 0:HV].rearrange("p (h t) -> p h t", t=B), ACT.Copy,
                                                scale=-1.0)
                last.then_inc(u12_done, 1)

            def solve(s, i):
                c = CPG * s + i
                rows = slice(C * (c % 2), C * (c % 2) + C)
                act.wait_ge(solve_done, c + 1)
                if c >= 2:
                    act.wait_ge(outs_done, c - 1)
                nc.scalar.activation(sol[rows, :], solve_ps[rows, :], ACT.Copy).then_inc(sol_done, 1)

            def gated(s, j):
                tile = TPG * s + j
                nc.scalar.preload_act_table_set(LN_EXP)
                act.wait_ge(rms_step, 3 * tile + 3)
                nc.scalar.activation(orms[:, :], oss[:, :], ACT.Ln, scale=1.0 / VD, bias=eps[:, 0:1]
                                     ).then_inc(rms_ln, 1)
                act.wait_ge(rms_ln, tile + 1)
                nc.scalar.activation(orms[:, :], orms[:, :], ACT.Exp, scale=-0.5).then_inc(rms_done, 1)

            def turn_o(s, j):
                tile = TPG * s + j
                ps = wait_ring(act, ("turn_o", s, j))
                if tile >= 1:
                    act.wait_ge(ring_done, ring_use[("mix", (tile - 1) // TPG, (tile - 1) % TPG)] + 1)
                nc.scalar.activation(oT[:, :, :], ps[:, 0:HV].rearrange("p (a t) -> p a t", a=2), ACT.Copy
                                     ).then_inc(ot_done, 1)

            def ln1(s, j):
                tile = TPG * s + j
                nc.scalar.preload_act_table_set(LN_EXP)
                act.wait_ge(ln_step, 3 * tile + 3)
                nc.scalar.activation(rstd[:, :], mv[:, 1:2], ACT.Ln, bias=eps[:, 0:1]).then_inc(ln_ln, 1)
                act.wait_ge(ln_ln, tile + 1)
                nc.scalar.activation(rstd[:, :], rstd[:, :], ACT.Exp, scale=-0.5).then_inc(rstd_done, 1)

            def split(s, j):
                tile = TPG * s + j
                ps = wait_ring(act, ("split", s, j))
                if tile >= 1:
                    act.wait_ge(ring_done, ring_use[("up", (tile - 1) // TPG, (tile - 1) % TPG)] + 1)
                nc.scalar.activation(xh[:, 0, :], ps[:, 0:P], ACT.Copy).then_inc(xh_done, 1)

            def up(s, j):
                tile = TPG * s + j
                ps = wait_ring(act, ("up", s, j))
                if tile >= 1:
                    act.wait_ge(ring_done, ring_use[("mid", (tile - 1) // TPG, (tile - 1) % TPG)] + 1)
                nc.scalar.activation(h1[:, 0, :], ps[:, :], ACT.Relu).then_inc(h_hi, 1)

            def mid(s, j):
                tile = TPG * s + j
                ps = wait_ring(act, ("mid", s, j))
                if tile >= 1:
                    act.wait_ge(ring_done, ring_use[("down", (tile - 1) // TPG, (tile - 1) % TPG)] + 1)
                nc.scalar.activation(h2[:, 0, :], ps[:, :], ACT.Relu).then_inc(h_hi, 1)

            def ln2(s, j):
                tile = TPG * s + j
                nc.scalar.preload_act_table_set(LN_EXP)
                act.wait_ge(y_step, 3 * tile + 3)
                nc.scalar.activation(rstd[:, :], mv[:, 1:2], ACT.Ln, bias=eps[:, 0:1]).then_inc(y_ln, 1)
                act.wait_ge(y_ln, tile + 1)
                nc.scalar.activation(rstd[:, :], rstd[:, :], ACT.Exp, scale=-0.5).then_inc(y_rstd, 1)

            do = {"proj": proj, "gate": gates, "decay": decay, "cross1": cross1, "cross2": cross2,
                  "solve": solve, "gated": gated, "turn_o": turn_o, "ln1": ln1, "split": split, "up": up, "mid": mid,
                  "ln2": ln2}
            for name, s, i in steps:
                if name == "logs":
                    logs(s)
                elif name == "cum":
                    cum()
                elif name in do:
                    do[name](s, i)

        @block.vector
        def _(dve):
            n_done = [0]

            def then_next(ins):
                n_done[0] += 1
                ins.then_inc(dve_done, 1)
                dve.wait_ge(dve_done, n_done[0])

            vec = nc.vector
            dve.wait_ge(ld_small, 16 * N_SMALL + 16)
            for n in range(2):
                vec.scalar_tensor_tensor(out=s_work[:, 2 * n:2 * n + 1], in0=s_in[:, n:n + 1], scalar=-1.0,
                                         in1=s_in[:, n:n + 1], op0=ALU.mult, op1=ALU.max)
                then_next(vec.tensor_scalar(s_work[:, 2 * n + 1:2 * n + 2], s_in[:, n:n + 1], 0.0, 2.0, ALU.is_ge,
                                            ALU.mult))
            vec.tensor_scalar(s_work[:, 1:2], s_work[:, 1:2], -1.0, None, ALU.add)
            then_next(vec.tensor_scalar(s_work[:, 3:4], s_work[:, 3:4], -1.0, 1.0 / 16, ALU.add, ALU.mult))
            then_next(vec.tensor_scalar(s_work[:, 4:5], s_work[:, 0:1], s_work[:, 2:3], 64.0, ALU.mult, ALU.mult))
            vec.tensor_scalar(s_work[:, 5:6], s_work[:, 4:5], s_in[:, 2:3], None, ALU.mult).then_inc(sgn_done, 1)

            dve.wait_ge(consts, 2)
            dve.wait_ge(z_ps, 1)
            then_next(vec.tensor_tensor(pre.rearrange("p (n k) -> p n k", k=2 * H),
                                        bank[4][:, 0:2 * NT * H].rearrange("p (n k) -> p n k", k=2 * H),
                                        bias_ab[:, :].unsqueeze(1).to_broadcast([P, NT, 2 * H]), ALU.add))
            vec.scalar_tensor_tensor(out=mag, in0=pre, scalar=-1.0, in1=pre, op0=ALU.mult, op1=ALU.min
                                     ).then_inc(mag_done, 1)
            dve.wait_ge(ld_w, 16 * N_W)
            for i in range(NP):
                m, w = i // 2, i % 2
                src = wqk_raw[:, w, m * P:(m + 1) * P] if m < H else wv_raw[:, w * P:(w + 1) * P]
                dve.wait_ge(ld_taps[2 * (m // HH) + w if m < H else 4], 16)
                tap = taps_qk[:, w, m * TAPS * P:(m + 1) * TAPS * P] if m < H else taps_v[:, w * TAPS * P:(w + 1) * TAPS * P]
                vec.tensor_tensor(w_taps[:, i, :, :].rearrange("p j c -> p c j"), over(src, TAPS),
                                  tap.rearrange("p (c j) -> p c j", j=TAPS), ALU.mult).then_inc(wtap_done, 1)
            dve.wait_ge(lnp_done, 1)
            pre_ab = pre.rearrange("p (n k) -> p n k", k=2 * H)
            lnp_ab = lnp.rearrange("p (n k) -> p n k", k=2 * H)
            g_v = g[:, :].rearrange("p (n h) -> p n h", h=H)
            lnb_v = lnb[:, :].rearrange("p (n h) -> p n h", h=H)
            then_next(vec.scalar_tensor_tensor(out=g_v, in0=pre_ab[:, :, 0:H], scalar=0.0, in1=lnp_ab[:, :, 0:H],
                                               op0=ALU.max, op1=ALU.add))
            dve.wait_ge(ea_done, 1)
            then_next(vec.scalar_tensor_tensor(out=g_v, in0=g_v, scalar=-1.0,
                                               in1=neg_a[:, :].unsqueeze(1).to_broadcast([P, NT, H]),
                                               op0=ALU.mult, op1=ALU.mult))
            then_next(vec.scalar_tensor_tensor(out=lnb_v, in0=pre_ab[:, :, H:2 * H], scalar=0.0,
                                               in1=lnp_ab[:, :, H:2 * H], op0=ALU.min, op1=ALU.subtract
                                               ))
            vec.tensor_scalar(lnb[:, :], lnb[:, :], LN2, None, ALU.add).then_inc(g_done, 1)

            def cum():
                dve.wait_ge(g_done, 1)
                dve.wait_ge(dg_done, 1)
                vec.tensor_tensor(lnb[:, :], lnb[:, :], bank[5][:, 0:P], ALU.subtract).then_inc(lnb_done, 1)

            def logs(s):
                dve.wait_ge(n2_done, 2 * H * (s + 1))
                if s >= 1:
                    dve.wait_ge(norms_done, s)
                    dve.wait_ge(cneg_done, s)
                vec.tensor_copy(n2_rows, norm_bank[0:2 * H, :]).then_inc(rows_done, 1)
                ps = wait_ring(dve, ("logs", s, 0))
                vec.tensor_scalar(lnn[:, :, :].rearrange("p w (n m) -> p w n m", m=H),
                                  ps[:, 0:2 * TPG * H].rearrange("p (n m w) -> p w n m", m=H, w=2),
                                  1e-12, None, ALU.max).then_inc(n2_max, 1)
                dve.wait_ge(log_done, s + 1)
                if s >= 1:
                    dve.wait_ge(dmask_done, TPG * s)
                dve.wait_ge(lnb_done, 1)
                vec.tensor_tensor(cneg[:, :], lnb[:, TPG * H * s:TPG * H * (s + 1)], lnn[:, 0, :], ALU.subtract
                                  ).then_inc(cneg_done, 1)

            def vals(s, jj):
                ps = wait_ring(dve, ("vals", s, jj))
                dve.wait_ge(norms_done, s + 1)
                if s >= 1:
                    dve.wait_ge(rhs_done, CPG * s)
                vec.tensor_tensor(nv[:, 2 * jj:2 * jj + 2, :].rearrange("p a (h v) -> p (a h) v", v=VD),
                                             ps[:, :].rearrange("p (h v) -> p h v", v=VD),
                                             over(norm_k[:, 2 * H * jj:2 * H * (jj + 1)], VD), ALU.mult
                                             ).then_inc(nv_done, 1)

            def decay(s, j):
                tile = TPG * s + j
                ps = wait_ring(dve, ("decay", s, j))
                dve.wait_ge(dmask_done, tile + 1)
                vec.tensor_tensor(dec[:, tile % 2], ps[:, :].rearrange("p (h t) -> p h t", t=C),
                                             dec[:, tile % 2], ALU.add).then_inc(darg_done, 1)

            def scores(s, i):
                j, hh = i // 2, i % 2
                tile = TPG * s + j
                hs = slice(HH * hh, HH * hh + HH)
                ps = wait_ring(dve, ("scores", s, i))[:, :].rearrange("p (h w t) -> p h w t", w=2, t=C)
                dve.wait_ge(dec_done, tile + 1)
                if s >= 1:
                    dve.wait_ge(unit_out, 16 * 4 * TPG * s)
                    dve.wait_ge(ring_done, ring_use[("cross1", s - 1, TPG - 1)] + 1)
                    dve.wait_ge(outs_done, CPG * s)
                vec.tensor_tensor(nmat[:, j, hs, :], ps[:, :, 0, :], dec[:, tile % 2, hs, :], ALU.mult)
                vec.tensor_tensor(amat[:, j, hs, :], ps[:, :, 1, :], dec[:, tile % 2, hs, :],
                                             ALU.mult).then_inc(scores_done, 1)

            def invert(s, t):
                base = 63 * s
                if t == 1:
                    dve.wait_ge(unit_in, 16 * (s + 1))
                    vec.memset(unit[:, :, :].rearrange("p i t -> p (i t)")[:, 0:B * B:B + 1], 1.0).then_inc(inv_step, 1)
                dve.wait_ge(inv_step, base + 2 * t - 1)
                cut = prod[:, 0:t * t].rearrange("p (r i) -> p r i", i=t)
                vec.tensor_tensor(cut, unit[:, 0:t, 0:t], unit[:, 0:t, t].unsqueeze(1).to_broadcast([P, t, t]),
                                  ALU.mult).then_inc(inv_step, 1)
                dve.wait_ge(inv_step, base + 2 * t)
                vec.tensor_reduce(unit[:, 0:t, t], cut, AX.X, ALU.add, negate=True).then_inc(inv_step, 1)

            def turn(s, j):
                tile = TPG * s + j
                dve.wait_ge(block_in[j], 16 * 4 * (s + 1))
                if tile >= 1:
                    dve.wait_ge(z21_done, tile)
                for a in range(2):
                    rows = slice(C * a, C * a + B)
                    last = vec.transpose(t11[rows], umat[rows, j, :, 0:B])
                last.then_inc(t11_done, 1)

            def keys(s, i):
                j, hh = i // 2, i % 2
                tile = TPG * s + j
                ps = wait_ring(dve, ("keys", s, i))
                dve.wait_ge(dend_done, tile + 1)
                if tile >= 2:
                    dve.wait_ge(state_mm, 2 * (tile - 1))
                vec.tensor_tensor(keyd[:, tile % 2, HH * hh:HH * hh + HH, :],
                                             ps[:, :].rearrange("p (h k) -> p h k", k=P),
                                             over(dend[:, j, HH * hh:HH * hh + HH], P), ALU.mult
                                             ).then_inc(keyd_done, 1)

            def read(s, i):
                c = CPG * s + i
                a, tile = c % 2, c // 2
                rows = slice(C * a, C * a + C)
                dve.wait_ge(read_done, c + 1)
                k_rows = slice(C * (1 - a), C * (2 - a))
                vec.tensor_tensor(heads(gpk[rows, :]), heads(read_ps[k_rows, :]),
                                  over(tile_heads(decay_kq[k_rows, a], tile), VD), ALU.mult).then_inc(gp_step, 1)
                vec.tensor_tensor(heads(gpq[rows, :]), heads(read_ps[rows, :]),
                                  over(tile_heads(decay_kq[rows, a], tile), VD), ALU.mult).then_inc(gp_step, 1)
                dve.wait_ge(gp_step, 2 * c + 1)
                dve.wait_ge(nv_done, TPG // 2 * (s + 1))
                if c >= 2:
                    dve.wait_ge(solve_done, c - 1)
                vec.tensor_tensor(rhs[rows, :], nv[rows, tile % TPG, :], gpk[rows, :], ALU.subtract
                                  ).then_inc(rhs_done, 1)

            def new_state(s, i):
                c = CPG * s + i
                dve.wait_ge(state_mm, c + 1)
                dve.wait_ge(stateg_done, c + 1)
                vec.tensor_tensor(state[:, (c + 1) % 2, :], state_ps, state_g[:, :], ALU.add).then_inc(state_done, 1)

            def outs(s, i):
                c = CPG * s + i
                tile = c // 2
                rows = slice(C * (c % 2), C * (c % 2) + C)
                dve.wait_ge(outs_done, c + 1)
                dve.wait_ge(gp_step, 2 * c + 2)
                if s >= 1:
                    dve.wait_ge(o_ready, tile - TPG + 1)
                    dve.wait_ge(ring_done, ring_use[("turn_o", s - 1, i // 2)] + 1)
                vec.tensor_tensor(o_t[rows, tile % TPG, :], outs_ps[rows, :], gpq[rows, :], ALU.add
                                  ).then_inc(o_done, 1)

            def rms(s, j):
                tile = TPG * s + j
                o = o_t[:, tile % TPG, :]
                dve.wait_ge(o_done, 2 * tile + 2)
                dve.wait_ge(norms_done, s + 1)
                vec.tensor_tensor(heads(o), heads(o), over(tile_heads(inv_q[s % 2], j), VD), ALU.mult
                                  ).then_inc(rms_step, 1)
                dve.wait_ge(rms_step, 3 * tile + 1)
                vec.tensor_tensor(osq[:, :], o, o, ALU.mult).then_inc(rms_step, 1)
                dve.wait_ge(rms_step, 3 * tile + 2)
                if tile >= 1:
                    dve.wait_ge(rms_done, tile)
                vec.tensor_reduce(oss[:, :], heads(osq[:, :]), AX.X, ALU.add).then_inc(rms_step, 1)

            def gated(s, j):
                tile = TPG * s + j
                o = o_t[:, tile % TPG, :]
                dve.wait_ge(gate_done, TPG // 2 * (s + 1))
                then_next(vec.tensor_tensor(o, o, gate[s % 2][:, j, :], ALU.mult))
                dve.wait_ge(rms_done, tile + 1)
                vec.tensor_tensor(heads(o), heads(o), over(orms[:, :], VD), ALU.mult).then_inc(o_ready, 1)

            def layer_stats(src, step_sem, base):
                vec.bn_stats(stats[:, :], src).then_inc(step_sem, 1)
                dve.wait_ge(step_sem, base + 2)
                vec.bn_aggr(mv[:, :], stats[:, :]).then_inc(step_sem, 1)

            def mix(s, j):
                tile = TPG * s + j
                ps = wait_ring(dve, ("mix", s, j))
                dve.wait_ge(xres_in[tile % 2], 16 * (tile // 2 + 1))
                vec.tensor_tensor(x1[:, :], ps[:, 0:P], xres[:, tile % 2, :], ALU.add
                                             ).then_inc(ln_step, 1)
                dve.wait_ge(ln_step, 3 * tile + 1)
                layer_stats(x1[:, :], ln_step, 3 * tile)

            def ln1(s, j):
                tile = TPG * s + j
                dve.wait_ge(ln_step, 3 * tile + 3)
                dve.wait_ge(rstd_done, tile + 1)
                vec.tensor_scalar(xn[:, j % 2, :], x1[:, :], mv[:, 0:1], rstd[:, 0:1], ALU.subtract, ALU.mult
                                  ).then_inc(xn_done, 1)

            def split(s, j):
                tile = TPG * s + j
                ps = wait_ring(dve, ("split", s, j))
                dve.wait_ge(xh_done, tile + 1)
                vec.tensor_tensor(xh[:, 1, :], ps[:, 0:P], xh[:, 0, :], ALU.subtract
                                             ).then_inc(xlo_done, 1)

            def hidden(name, s, j, buf):
                ps = wait_ring(dve, (name, s, j))
                dve.wait_ge(h_hi, 2 * (TPG * s + j) + (2 if name == "mid" else 1))
                vec.scalar_tensor_tensor(out=buf[:, 1, :], in0=ps[:, :], scalar=0.0, in1=buf[:, 0, :],
                                                    op0=ALU.max, op1=ALU.subtract).then_inc(h_lo, 1)

            def down(s, j):
                tile = TPG * s + j
                ps = wait_ring(dve, ("down", s, j))
                vec.scalar_tensor_tensor(out=x3[:, :], in0=ps[:, 0:P], scalar=s_work[:, 5:6],
                                                    in1=xn[:, tile % 2, :], op0=ALU.mult, op1=ALU.add
                                                    ).then_inc(y_step, 1)
                dve.wait_ge(y_step, 3 * tile + 1)
                layer_stats(x3[:, :], y_step, 3 * tile)

            def ln2(s, j):
                tile = TPG * s + j
                dve.wait_ge(y_step, 3 * tile + 3)
                dve.wait_ge(y_rstd, tile + 1)
                if tile >= 2:
                    dve.wait_ge(stored[tile % 2], 16 * (tile // 2))
                vec.tensor_scalar(fin[:, tile % 2, :], x3[:, :], mv[:, 0:1], rstd[:, 0:1], ALU.subtract, ALU.mult
                                  ).then_inc(fin_done, 1)

            do = {"decay": decay, "scores": scores, "invert": invert, "turn": turn, "keys": keys,
                  "read": read, "state": new_state, "outs": outs, "rms": rms, "gated": gated, "mix": mix, "ln1": ln1,
                  "split": split, "down": down, "ln2": ln2,
                  "vals": vals}
            for name, s, i in steps:
                if name == "logs":
                    logs(s)
                elif name == "cum":
                    cum()
                elif name in ("up", "mid"):
                    hidden(name, s, i, h1 if name == "up" else h2)
                elif name in do:
                    do[name](s, i)

        @block.tensor
        def _(pe):
            mm = nc.tensor.matmul
            pe.wait_ge(consts, 1)
            for q in range(4):
                pe.wait_ge(ld_x[q], 16)
                for n in range(4):
                    last = nc.tensor.transpose(bank[q][:, n * P:(n + 1) * P], x_in[:, 4 * q + n, :], ident[:, :])
                last.then_inc(xt_ps, 1)
            pe.wait_ge(ld_small, 16 * N_SMALL + 16)
            for n in range(NT):
                if n % 4 == 0:
                    pe.wait_ge(xt_done, n // 4 + 1)
                last = mm(bank[4][:, n * 2 * H:(n + 1) * 2 * H], xT[:, TAPS - 1 + n * P:TAPS - 1 + (n + 1) * P], wab[:, :],
                          start=True, stop=True)
            last.then_inc(z_ps, 1)
            def cum():
                pe.wait_ge(consts, 2)
                pe.wait_ge(g_done, 1)
                mm(bank[5][:, 0:P], upto, g[:, :], start=True, stop=True)
                for a in range(2):
                    mm(bank[5][:, P * (1 + a):P * (2 + a)], tri_kq[:, a, :, :].rearrange("p w t -> p (w t)"), g[:, :],
                       start=True, stop=True)
                for a in range(2):
                    last = mm(bank[6][:, P * a:P * (1 + a)], in_chunk[:, a, :], g[:, :], start=True, stop=True)
                last.then_inc(cum_ps, 1)

            def take_ring(step):
                n = ring_use[step]
                if n >= 3:
                    pe.wait_ge(*bank_read(ring_steps[n - 3]))
                elif n == 2:
                    pe.wait_ge(dg_done, 1)
                return ring_bank[n % 3]

            def taps_of(s, i, js):
                for j in js:
                    last = mm(proj_bank[i % 2][:, :], w_taps[:, i, j, :], xT[:, s * GT + j:(s + 1) * GT + j],
                              start=(j == 0), stop=(j == TAPS - 1))
                return last

            def begin(s, i):
                n = NP * s + i
                if n >= 2:
                    pe.wait_ge(silu_done, n - 1)
                if s == 0:
                    pe.wait_ge(wtap_done, i + 1)
                taps_of(s, i, range(TAPS // 2))

            def proj(s, i):
                taps_of(s, i, range(TAPS // 2, TAPS)).then_inc(proj_done, 1)

            def norm2(s, i):
                n = 2 * H * s + i
                if i == 0 and s > 0:
                    pe.wait_ge(rows_done, s)
                pe.wait_ge(sq_done, n + 1)
                mm(norm_bank[0:2 * H, :], pick[:, 2 * H - 1 - i:4 * H - 1 - i], sq[:, i % 2, :],
                   start=(i == 0), stop=(i == 2 * H - 1)).then_inc(n2_done, 1)

            def logs(s, _):
                ps = take_ring(("logs", s, 0))
                pe.wait_ge(rows_done, s + 1)
                for j in range(TPG):
                    last = nc.tensor.transpose(ps[:, j * 2 * H:(j + 1) * 2 * H], n2_rows[:, j * P:(j + 1) * P],
                                               ident[0:2 * H, 0:2 * H])
                last.then_inc(ring_done, 1)

            def gates(s, jj):
                ps = take_ring(("gate", s, jj))
                for a in range(2):
                    t0 = TAPS - 1 + s * GT + (2 * jj + a) * P
                    last = mm(ps[:, a * HV:(a + 1) * HV], xT[:, t0:t0 + P], wg[:, :], start=True, stop=True)
                last.then_inc(ring_done, 1)

            def vals(s, jj):
                ps = take_ring(("vals", s, jj))
                pe.wait_ge(silu_done, NP * (s + 1))
                for a in range(2):
                    for w in range(2):
                        last = nc.tensor.transpose(ps[:, a * HV + w * P:a * HV + (w + 1) * P],
                                                   vT[:, w, (2 * jj + a) * P:(2 * jj + a + 1) * P], ident[:, :])
                last.then_inc(ring_done, 1)

            def decay(s, j):
                ps = take_ring(("decay", s, j))
                pe.wait_ge(gtri_done, TPG * s + j + 1)
                mm(ps[:, :], same_chunk[:, :], g_tri[:, :, :].rearrange("p h t -> p (h t)"), start=True, stop=True
                   ).then_inc(ring_done, 1)

            def scores(s, i):
                j, hh = i // 2, i % 2
                ps = take_ring(("scores", s, i))
                for h in range(HH):
                    for a in range(2):
                        tile_kq = kq[s % 2][:, HH * hh + h, j, :]
                        k_cols = tile_kq[:, C * (1 + a):C * (2 + a)]
                        q_cols = tile_kq[:, 3 * C * a:3 * C * a + C]
                        dst = ps[a * C:(a + 1) * C, h * 2 * C:(h + 1) * 2 * C]
                        mm(dst[:, 0:C], k_cols, k_cols, start=True, stop=True)
                        last = mm(dst[:, C:2 * C], k_cols, q_cols, start=True, stop=True)
                last.then_inc(ring_done, 1)

            def cross1(s, j):
                ps = take_ring(("cross1", s, j))
                pe.wait_ge(t11_done, TPG * s + j + 1)
                for a in range(2):
                    src, dst = slice(C * a, C * a + B), slice(C * a + B, C * a + C)
                    for h in range(H):
                        last = mm(ps[dst, h * B:(h + 1) * B], nmat[src, j, h, B:C], t11[src, h, :],
                                  start=True, stop=True)
                last.then_inc(ring_done, 1)

            def cross2(s, j):
                ps = take_ring(("cross2", s, j))
                pe.wait_ge(z21_done, TPG * s + j + 1)
                for a in range(2):
                    src, dst = slice(C * a + B, C * a + C), slice(C * a, C * a + B)
                    for h in range(H):
                        last = mm(ps[dst, h * B:(h + 1) * B], z21[src, h, :], umat[src, j, h, B:C],
                                  start=True, stop=True)
                last.then_inc(ring_done, 1)

            def keys(s, i):
                j, hh = i // 2, i % 2
                ps = take_ring(("keys", s, i))
                for h in range(HH):
                    last = nc.tensor.transpose(ps[:, h * P:(h + 1) * P],
                                               kq[s % 2][:, HH * hh + h, j, C:3 * C], ident[:, :])
                last.then_inc(ring_done, 1)

            def read_heads(s, i, hs):
                c = CPG * s + i
                for h in hs:
                    last = mm(read_ps[:, h * VD:(h + 1) * VD], kq[s % 2][:, h, i // 2, i % 2 * P:(i % 2 + 1) * P],
                              state[:, c % 2, h * VD:(h + 1) * VD], start=True, stop=True)
                return last

            def read_half(s, i):
                c = CPG * s + i
                if c > 0:
                    pe.wait_ge(state_done, c)
                read_heads(s, i, range(HH))

            def read(s, i):
                read_heads(s, i, range(HH, H)).then_inc(read_done, 1)

            def solve(s, i):
                c = CPG * s + i
                rows = slice(C * (c % 2), C * (c % 2) + C)
                pe.wait_ge(rhs_done, c + 1)
                pe.wait_ge(u12_done, c // 2 + 1)
                if c >= 1:
                    pe.wait_ge(o_done, c)
                for h in range(H):
                    last = mm(solve_ps[rows, h * VD:(h + 1) * VD], umat[rows, i // 2, h, :],
                              rhs[rows, h * VD:(h + 1) * VD], start=True, stop=True)
                last.then_inc(solve_done, 1)

            def state_heads(s, i, hs):
                c = CPG * s + i
                rows = slice(C * (c % 2), C * (c % 2) + C)
                for h in hs:
                    last = mm(state_ps[:, h * VD:(h + 1) * VD], keyd[rows, c // 2 % 2, h, :],
                              sol[rows, h * VD:(h + 1) * VD], start=True, stop=True)
                return last

            def state_half(s, i):
                c = CPG * s + i
                pe.wait_ge(sol_done, c + 1)
                pe.wait_ge(gp_step, 2 * c + 2)
                pe.wait_ge(keyd_done, 2 * (c // 2) + 2)
                state_heads(s, i, range(HH))

            def new_state(s, i):
                state_heads(s, i, range(HH, H)).then_inc(state_mm, 1)

            def outs(s, i):
                c = CPG * s + i
                rows = slice(C * (c % 2), C * (c % 2) + C)
                for h in range(H):
                    last = mm(outs_ps[rows, h * VD:(h + 1) * VD], amat[rows, i // 2, h, :],
                              sol[rows, h * VD:(h + 1) * VD], start=True, stop=True)
                last.then_inc(outs_done, 1)

            def turn_o(s, j):
                tile = TPG * s + j
                ps = take_ring(("turn_o", s, j))
                pe.wait_ge(o_ready, tile + 1)
                for w in range(2):
                    last = nc.tensor.transpose(ps[:, w * P:(w + 1) * P], o_t[:, tile % TPG, w * P:(w + 1) * P], ident[:, :])
                last.then_inc(ring_done, 1)

            def mix(s, j):
                tile = TPG * s + j
                ps = take_ring(("mix", s, j))
                pe.wait_ge(ot_done, tile + 1)
                for w in range(2):
                    last = mm(ps[:, 0:P], oT[:, w, :], wo[:, w, :], start=(w == 0), stop=(w == 1))
                last.then_inc(ring_done, 1)

            def split(s, j):
                ps = take_ring(("split", s, j))
                pe.wait_ge(xn_done, TPG * s + j + 1)
                nc.tensor.transpose(ps[:, 0:P], xn[:, j % 2, :], ident[:, :]).then_inc(ring_done, 1)

            def up(s, j):
                ps = take_ring(("up", s, j))
                pe.wait_ge(xlo_done, TPG * s + j + 1)
                pe.wait_ge(mlpw_done, 2)
                for f in range(4):
                    cols = slice(f * P, (f + 1) * P)
                    for part in range(2):
                        last = mm(ps[:, cols], w0[:, cols], xh[:, part, :], start=(part == 0), stop=(part == 1))
                last.then_inc(ring_done, 1)

            def mid(s, j):
                ps = take_ring(("mid", s, j))
                pe.wait_ge(h_lo, 2 * (TPG * s + j) + 1)
                for f in range(4):
                    cols = slice(f * P, (f + 1) * P)
                    for k in range(4):
                        for part in range(2):
                            last = mm(ps[:, cols], w1[:, k, cols], h1[:, part, k * P:(k + 1) * P],
                                      start=(k == 0 and part == 0), stop=(k == 3 and part == 1))
                last.then_inc(ring_done, 1)

            def down(s, j):
                ps = take_ring(("down", s, j))
                pe.wait_ge(h_lo, 2 * (TPG * s + j) + 2)
                for k in range(4):
                    for part in range(2):
                        last = mm(ps[:, 0:P], h2[:, part, k * P:(k + 1) * P], w2[:, k, :],
                                  start=(k == 0 and part == 0), stop=(k == 3 and part == 1))
                last.then_inc(ring_done, 1)

            do = {"begin": begin, "proj": proj, "norm2": norm2, "logs": logs, "gate": gates, "vals": vals, "decay": decay, "scores": scores,
                  "cross1": cross1, "cross2": cross2, "keys": keys, "read_half": read_half, "read": read, "solve": solve,
                  "state_half": state_half, "state": new_state, "outs": outs, "turn_o": turn_o, "mix": mix, "split": split, "up": up, "mid": mid, "down": down}
            for name, s, i in steps:
                if name == "cum":
                    cum()
                elif name in do:
                    do[name](s, i)


_NAMES = ("L0_attn_x L0_attn_Wq L0_attn_Wk L0_attn_Wv L0_attn_Wa L0_attn_Wb L0_attn_Wg L0_attn_Wo L0_attn_A_log "
          "L0_attn_dt_bias L0_attn_conv_q L0_attn_conv_k L0_attn_conv_v L0_attn_o_norm_w L0_ffn_k0 L0_ffn_k1 "
          "L0_ffn_k2 L0_ffn_s0 L0_ffn_s1 L0_ffn_s2").split()


def kernel(**inputs):
    import numpy as np
    import concourse.bacc as bacc
    from concourse.bass_utils import run_bass_kernel_spmd

    nc = bacc.Bacc("TRN2", target_bir_lowering=False, num_devices=1)
    arrays, args = {}, []
    for name in _NAMES:
        a = np.ascontiguousarray(inputs[name])
        if name == "L0_attn_x":
            a = a.reshape(a.shape[1:])
        if a.ndim == 0:
            a = a.reshape(1)
        arrays[f"in_{name}"] = a
        args.append(nc.dram_tensor(f"in_{name}", a.shape, mybir.dt.from_np(a.dtype), kind="ExternalInput").ap())
    T, D = arrays["in_L0_attn_x"].shape
    args.append(nc.dram_tensor("out", (T, D), F32, kind="ExternalOutput").ap())
    post_ln_block(nc, *args)
    r = run_bass_kernel_spmd(nc, [arrays], core_ids=[0])
    return r.results[0]["out"].reshape(1, T, D)
```
